# Optimizing a Trainium2 kernel written in Bass

```python
import numpy as np
import jax
import jax.numpy as jnp

def _softmax(x, axis=-1):
    return jax.nn.softmax(x, axis=axis)

def _gelu(x):
    return jax.nn.gelu(x, approximate=True)

def _silu(x):
    return jax.nn.silu(x)

def _sigmoid(x):
    return jax.nn.sigmoid(x)

def _layernorm(x, axis=-1, eps=1e-05):
    m = jnp.mean(x, axis=axis, keepdims=True)
    v = jnp.var(x, axis=axis, keepdims=True)
    return (x - m) / jnp.sqrt(v + eps)

def _scatter_add(tgt, idx, src, axis=0):
    return tgt.at[idx].add(src)

def _segment_sum(src, seg, n):
    return jax.ops.segment_sum(src, seg, n)
kernel_name = 'mk_lm_tower_d1_tok_ids512_r4_483175'

def setup_inputs(seed: int=0):
    np.random.seed(seed)
    _w = jnp.asarray

    def _rec_inputs():
        import jax
        import jax.numpy as jnp
        _rk = jax.random.key(seed)
        x = jax.random.randint(jax.random.fold_in(_rk, 1), (2, 1024), 0, 125, jnp.int32)
        return x
    x = _rec_inputs()

    def _L0_tok_setup():
        import jax, jax.numpy as jnp
        import numpy as np
        VOCAB = 125
        DIM = 128
        CONTEXT = 2
        GROUPS = DIM // 4
        key = jax.random.key(seed)
        k1, k2, k3 = jax.random.split(key, 3)
        y = jax.random.randint(k1, (64, 512), 0, VOCAB, dtype=jnp.int64)
        emb_table = jax.random.normal(k2, (VOCAB, DIM), dtype=jnp.float32)
        conv_w = jax.random.normal(k3, (DIM, DIM // GROUPS, CONTEXT), dtype=jnp.float32) * 0.1
        return {'y': y, 'emb_table': emb_table, 'conv_w': conv_w}
    _L0_tok_all = _L0_tok_setup()
    _L0_tok_in = {k: v for k, v in _L0_tok_all.items() if k in ('emb_table', 'conv_w')}
    del _L0_tok_all

    def _L0_attn_setup():
        import jax, jax.numpy as jnp
        import numpy as np
        DIM = 128
        HEADS = 8
        DIM_HEAD = 64
        INNER = HEADS * DIM_HEAD
        key = jax.random.key(seed)
        kx, kq, kk, kv, ko = jax.random.split(key, 5)
        x = jax.random.normal(kx, (2, 1024, DIM), dtype=jnp.float32)
        lim = float(np.sqrt(6.0 / (DIM + INNER)))
        Wq = jax.random.uniform(kq, (INNER, DIM), minval=-lim, maxval=lim, dtype=jnp.float32)
        Wk = jax.random.uniform(kk, (INNER, DIM), minval=-lim, maxval=lim, dtype=jnp.float32)
        Wv = jax.random.uniform(kv, (INNER, DIM), minval=-lim, maxval=lim, dtype=jnp.float32) * 0.67
        lim_o = float(np.sqrt(6.0 / (INNER + DIM)))
        Wo = jax.random.uniform(ko, (DIM, INNER), minval=-lim_o, maxval=lim_o, dtype=jnp.float32) * 0.67
        return {'x': x, 'Wq': Wq, 'Wk': Wk, 'Wv': Wv, 'Wo': Wo}
    _L0_attn_all = _L0_attn_setup()
    _L0_attn_in = {k: v for k, v in _L0_attn_all.items() if k in ('Wq', 'Wk', 'Wv', 'Wo')}
    del _L0_attn_all

    def _L0_ffn_setup():
        import jax, jax.numpy as jnp
        import numpy as np
        MICRO_BATCHES = 2
        TOP_K = 2
        D = 128
        E = 8
        B, S = (8, 2048)
        key = jax.random.key(seed)
        ks = jax.random.split(key, 12)
        s = 0.02
        return {'x': jax.random.normal(ks[0], (B, S, D), dtype=jnp.float32), 'ln_g': jnp.ones((D,), jnp.float32), 'ln_b': jnp.zeros((D,), jnp.float32), 'attn_w': jax.random.normal(ks[1], (D, D), jnp.float32) * s, 'attn_b': jnp.zeros((D,), jnp.float32), 'gate_w': jax.random.normal(ks[2], (E, D), jnp.float32) * s, 'fc1_w': jax.random.normal(ks[3], (E, 4 * D, D), jnp.float32) * s, 'fc1_b': jnp.zeros((E, 4 * D), jnp.float32), 'fc2_w': jax.random.normal(ks[4], (E, D, 4 * D), jnp.float32) * s, 'fc2_b': jnp.zeros((E, D), jnp.float32), 'next_w': jax.random.normal(ks[5], (D, D), jnp.float32) * s, 'next_b': jnp.zeros((D,), jnp.float32)}
    _L0_ffn_all = _L0_ffn_setup()
    _L0_ffn_in = {k: v for k, v in _L0_ffn_all.items() if k in ('ln_g', 'ln_b', 'attn_w', 'attn_b', 'gate_w', 'fc1_w', 'fc1_b', 'fc2_w', 'fc2_b', 'next_w', 'next_b')}
    del _L0_ffn_all
    return {'x': x, 'L0_tok_emb_table': _L0_tok_in['emb_table'], 'L0_tok_conv_w': _L0_tok_in['conv_w'], 'L0_attn_Wq': _L0_attn_in['Wq'], 'L0_attn_Wk': _L0_attn_in['Wk'], 'L0_attn_Wv': _L0_attn_in['Wv'], 'L0_attn_Wo': _L0_attn_in['Wo'], 'L0_ffn_ln_g': _L0_ffn_in['ln_g'], 'L0_ffn_ln_b': _L0_ffn_in['ln_b'], 'L0_ffn_attn_w': _L0_ffn_in['attn_w'], 'L0_ffn_attn_b': _L0_ffn_in['attn_b'], 'L0_ffn_gate_w': _L0_ffn_in['gate_w'], 'L0_ffn_fc1_w': _L0_ffn_in['fc1_w'], 'L0_ffn_fc1_b': _L0_ffn_in['fc1_b'], 'L0_ffn_fc2_w': _L0_ffn_in['fc2_w'], 'L0_ffn_fc2_b': _L0_ffn_in['fc2_b'], 'L0_ffn_next_w': _L0_ffn_in['next_w'], 'L0_ffn_next_b': _L0_ffn_in['next_b']}

def reference(x, L0_tok_emb_table, L0_tok_conv_w, L0_attn_Wq, L0_attn_Wk, L0_attn_Wv, L0_attn_Wo, L0_ffn_ln_g, L0_ffn_ln_b, L0_ffn_attn_w, L0_ffn_attn_b, L0_ffn_gate_w, L0_ffn_fc1_w, L0_ffn_fc1_b, L0_ffn_fc2_w, L0_ffn_fc2_b, L0_ffn_next_w, L0_ffn_next_b):
    import jax
    import jax.numpy as jnp

    def _L0_tok_ref(y, emb_table, conv_w):
        import jax, jax.numpy as jnp
        import numpy as np
        VOCAB = 125
        DIM = 128
        CONTEXT = 2
        GROUPS = DIM // 4
        mask = y >= 0
        emb = emb_table[jnp.clip(y, 0)] * mask[..., None].astype(emb_table.dtype)
        x = jnp.transpose(emb, (0, 2, 1))
        x = jnp.pad(x, ((0, 0), (0, 0), (CONTEXT - 1, 0)))
        out = jax.lax.conv_general_dilated(x, conv_w, window_strides=(1,), padding='VALID', dimension_numbers=('NCH', 'OIH', 'NCH'), feature_group_count=GROUPS)
        out = jnp.transpose(out, (0, 2, 1))
        return jax.nn.relu(out)

    def _L0_attn_ref(x, Wq, Wk, Wv, Wo):
        import jax, jax.numpy as jnp
        import numpy as np
        DIM = 128
        HEADS = 8
        DIM_HEAD = 64
        INNER = HEADS * DIM_HEAD
        scale = DIM_HEAD ** (-0.5)
        b, n, _ = x.shape

        def proj(W):
            t = jnp.einsum('bnc,ec->bne', x, W)
            return t.reshape(b, n, HEADS, DIM_HEAD).transpose(0, 2, 1, 3)
        q, k, v = (proj(Wq), proj(Wk), proj(Wv))
        dots = jnp.einsum('bhqd,bhkd->bhqk', q, k) * scale
        attn = jax.nn.softmax(dots, axis=-1)
        out = jnp.einsum('bhqk,bhkd->bhqd', attn, v)
        out = out.transpose(0, 2, 1, 3).reshape(b, n, INNER)
        out = jnp.einsum('bne,ce->bnc', out, Wo)
        return out + x

    def _L0_ffn_ref(x, ln_g, ln_b, attn_w, attn_b, gate_w, fc1_w, fc1_b, fc2_w, fc2_b, next_w, next_b):
        import jax, jax.numpy as jnp
        import numpy as np
        MICRO_BATCHES = 2
        TOP_K = 2
        D = 128
        E = 8
        B, S = (8, 2048)
        b, s, d = x.shape
        xf = x.reshape(b * s, d)
        mu = jnp.mean(xf, axis=-1, keepdims=True)
        var = jnp.var(xf, axis=-1, keepdims=True)
        normed = (xf - mu) / jnp.sqrt(var + 1e-05) * ln_g + ln_b
        x_attn = normed @ attn_w.T + attn_b + xf
        logits = x_attn @ gate_w.T
        _scores, _indices = jax.lax.top_k(logits, TOP_K)
        e = fc1_w.shape[0]
        t = b * s // (MICRO_BATCHES * e)
        tok = x_attn.reshape(MICRO_BATCHES, e, t, d)
        h = jnp.einsum('meti,ehi->meth', tok, fc1_w) + fc1_b[None, :, None, :]
        h = jax.nn.gelu(h, approximate=False)
        y = jnp.einsum('meth,edh->metd', h, fc2_w) + fc2_b[None, :, None, :]
        yf = y.reshape(b * s, d)
        out = jax.nn.gelu(yf @ next_w.T + next_b, approximate=False)
        return out.reshape(b, s, d)
    h = _L0_tok_ref(x, L0_tok_emb_table, L0_tok_conv_w)
    h = h + _L0_attn_ref(_layernorm(h, axis=-1), L0_attn_Wq, L0_attn_Wk, L0_attn_Wv, L0_attn_Wo)
    h = h + _L0_ffn_ref(_layernorm(h, axis=-1), L0_ffn_ln_g, L0_ffn_ln_b, L0_ffn_attn_w, L0_ffn_attn_b, L0_ffn_gate_w, L0_ffn_fc1_w, L0_ffn_fc1_b, L0_ffn_fc2_w, L0_ffn_fc2_b, L0_ffn_next_w, L0_ffn_next_b)
    return h

_drawn_inputs = setup_inputs


def setup_inputs(seed=0):
    import zlib

    import numpy as np

    out = dict(_drawn_inputs(seed))
    spreads = {'L0_ffn_ln_g': (1.0, 0.6),
     'L0_ffn_ln_b': (0.0, 0.8),
     'L0_ffn_attn_b': (0.0, 0.8),
     'L0_ffn_fc1_b': (0.0, 0.8),
     'L0_ffn_fc2_b': (0.0, 0.8),
     'L0_ffn_next_b': (0.0, 0.8)}
    factors = {'L0_attn_Wq': 3.886,
     'L0_attn_Wk': 3.827,
     'L0_ffn_attn_w': 8.0,
     'L0_ffn_fc1_w': 8.0,
     'L0_ffn_fc2_w': 8.0,
     'L0_ffn_next_w': 5.117}
    for name, (base, spread) in spreads.items():
        noise = np.random.default_rng([zlib.crc32(name.encode()), seed]).standard_normal(out[name].shape)
        drawn = base * np.exp(spread * noise) if base else spread * noise
        out[name] = jnp.asarray(drawn.astype(out[name].dtype))
    for name, factor in factors.items():
        out[name] = (out[name] * factor).astype(out[name].dtype)
    return out
```

```python
from contextlib import ExitStack

import concourse.bass as bass
from concourse import mybir

F32 = mybir.dt.float32
F32R = mybir.dt.float32r
BF16 = mybir.dt.bfloat16
I32 = mybir.dt.int32
ALU = mybir.AluOpType
ACT = mybir.ActivationFunctionType
AX = mybir.AxisListType

C = 128
B, S = 2, 1024
HEADS, D = 8, 64
PAIRS = HEADS // 2
STEPS = B * PAIRS
CHUNK = 128
NCH = B * S // CHUNK
KCH = S // CHUNK
GROUP = 4
NG = NCH // GROUP
E, HID = 8, 512
HC = HID // 128
TAPS = 2
EPS = 1e-5
SCALE = float(D) ** -0.5
BANK = 512
SLOTS = 3
QUARTERS = 4


def prologue_order():
    order = [("q", 0), ("k", 0), ("q", 1), ("k", 1)]
    for h in range(2):
        order += [("max", h, qc) for qc in range(KCH)] + [("row", h)]
    return order


def step_order(prepare):
    maxes = [("max", h, qc) for h in range(2) for qc in range(KCH)]
    between = {0: [("q", 0), ("k", 0)], 1: [("q", 1), ("k", 1)]}
    at = 0
    for kc, n in zip(range(2, KCH), (3, 3, 3, 3, 2, 2)):
        between[kc] = maxes[at:at + n]
        at += n
    between[5] = [("row", 0)] + between[5]
    order = []
    for kc in range(KCH):
        extra = between[kc] if prepare else []
        order += [("exp", kc, 0)] + extra[:1] + [("exp", kc, 1)] + extra[1:]
        if kc:
            order.append(("pv", kc - 1))
    if prepare:
        order.append(("row", 1))
    return order + [("pv", KCH - 1), ("den",)]


PROLOGUE = prologue_order()
ITEMS = len([i for i in step_order(True) if i[0] != "pv"])
assert ITEMS % SLOTS == 0


def numbered(prologue, prepare=True):
    n = 0
    for item in (PROLOGUE if prologue else step_order(prepare)):
        if item[0] == "pv":
            yield item, None
        else:
            yield item, n
            n += 1


def item_count(s, n):
    return n + 1 if s is None else s * ITEMS + (len(PROLOGUE) + n + 1)


def slot_of(s_prologue, n):
    return (n if s_prologue else len(PROLOGUE) + n) % SLOTS


def adds_before_reuse(kc):
    return kc - 1 if kc < 2 else max(kc - 2, 1)


def build(nc, x, emb, conv_w, wq, wk, wv, wo, ln_g, ln_b, attn_w, attn_b,
          fc1_w, fc1_b, fc2_w, fc2_b, next_w, next_b, out):
    VOCAB = emb.shape[0]
    with ExitStack() as ctx:
        def sem(name):
            return ctx.enter_context(nc.semaphore(name))

        def sb(name, shape, dt=F32, scope=ctx):
            return scope.enter_context(nc.sbuf_tensor(name, shape, dt))

        slots = [ctx.enter_context(nc.psum_tensor(f"slot{i}", [128, 2 * BANK], F32)) for i in range(SLOTS)]
        acc_o = ctx.enter_context(nc.psum_tensor("acc_o", [128, 2 * BANK], F32))

        def bank(k):
            t = slots[k // 2] if k < 2 * SLOTS else acc_o
            return t[:, (k % 2) * BANK:(k % 2 + 1) * BANK]

        ident = sb("ident", [128, 128])
        ones64 = sb("ones64", [128, D])
        iota_i = sb("iota_i", [128, 1], I32)
        iota_f = sb("iota_f", [128, 1])
        eps = sb("eps", [128, 1])
        group_mask = sb("group_mask", [128, 32])
        chunk_mask = sb("chunk_mask", [KCH, KCH, CHUNK], BF16)
        woT = sb("woT", [128, PAIRS, C])
        small = sb("small", [128, 2 * C + 43])
        next_b_row = sb("next_b_row", [128, C])
        stats = sb("stats", [128, GROUP, 6])
        mv = sb("mv", [128, GROUP, 2])
        std = sb("std", [128, GROUP])
        rstd = sb("rstd", [128, GROUP])
        residual = sb("residual", [128, NCH, C])
        attn_out = sb("attn_out", [128, STEPS, S])
        v_all = sb("v_all", [128, STEPS, KCH, 2 * D])

        with ExitStack() as front:
            emb_sb = sb("emb_sb", [VOCAB, C], F32, front)
            conv_sb = sb("conv_sb", [C, 4, TAPS], F32, front)
            conv_diag = sb("conv_diag", [C, TAPS, C], F32, front)
            embT = sb("embT", [C, VOCAB], F32, front)
            convT = sb("convT", [C, TAPS * C], F32, front)
            folded = sb("folded", [VOCAB, TAPS * C], F32, front)
            wvR = sb("wvR", [C, HEADS * D], F32R, front)
            wvL = sb("wvL", [C, HEADS * D], F32R, front)
            raw_small = sb("raw_small", [128, 2, C], F32, front)
            raw_bias = sb("raw_bias", [43, C], F32, front)
        with ExitStack() as att:
            sums = [sb(f"sums{h}", [128, S], F32, att) for h in range(2)]
            den_sb = sb("den_sb", [128, S], F32, att)
            o_sb = sb("o_sb", [128, S], F32, att)
            wqk = sb("wqk", [C, PAIRS, 2, 2 * D], F32, att)
            xR = sb("xR", [C, B * S], F32R, att)
            xL = sb("xL", [C, B * S], F32R, att)
            w_stR = sb("w_stR", [C, 4, 2, D], F32R, att)
            w_stL = sb("w_stL", [C, 4, 2, D], F32R, att)
            q_full = [[sb(f"q_full{p}{h}", [128, S], F32R, att) for h in range(2)] for p in range(2)]
            q_max = [[sb(f"q_max{p}{h}", [128, S], F32R, att) for h in range(2)] for p in range(2)]
            k_round = [[sb(f"k_round{p}{h}", [128, S], F32R, att) for h in range(2)] for p in range(2)]
            k_rest = [[sb(f"k_rest{p}{h}", [128, S], F32R, att) for h in range(2)] for p in range(2)]
            v_st = [sb(f"v_st{p}", [128, KCH, 2 * D], F32, att) for p in range(2)]
            probs = [[sb(f"probs{h}{i}", [128, S], F32, att) for i in range(2)] for h in range(2)]
            maxes = [sb(f"maxes{h}", [128, KCH], F32, att) for h in range(2)]
        fc1T = sb("fc1T", [128, E, HC, C])
        fc2T = sb("fc2T", [128, E, HC, C])
        normed2 = sb("normed2", [128, NCH, C])
        h1n = sb("h1n", [128, NCH, C])
        normT = [sb(f"normT{i}", [128, BANK]) for i in range(2)]
        xaT = sb("xaT", [C, B * S])
        hidT = [sb(f"hidT{i}", [128, HC, B * CHUNK]) for i in range(2)]
        yT = [sb(f"yT{i}", [C, B * CHUNK]) for i in range(2)]
        z_pre = [sb(f"z_pre{i}", [128, B, C]) for i in range(2)]
        z_act = [sb(f"z_act{i}", [128, B, C]) for i in range(2)]
        out_sb = [sb(f"out_sb{i}", [128, B, C]) for i in range(2)]

        flat = attn_out[:, :, :].rearrange("p s n -> p (s n)")
        h0 = flat[:, 0:NCH * C].rearrange("p (t c) -> p t c", c=C)
        x1 = flat[:, NCH * C:2 * NCH * C].rearrange("p (t c) -> p t c", c=C)
        PAD = 2 * NCH * C
        onehot = flat[0:VOCAB, PAD:PAD + B * (S + 1)].rearrange("p (b n) -> p b n", b=B)
        ids = residual[0:VOCAB, :, :].bitcast(I32).rearrange("p t c -> p (t c)")
        vflat = v_all[:, :, :, :].rearrange("p s k d -> p (s k d)")
        raw_w = vflat[:, 0:3 * PAIRS * C].rearrange("p (w r c) -> p w r c", w=3, c=C)
        raw_wo = vflat[:, 3 * PAIRS * C:4 * PAIRS * C].rearrange("p (r c) -> p r c", c=C)
        FCN = E * HC * C
        raw_fc1 = vflat[:, 0:FCN].rearrange("p (e r c) -> p e r c", e=E, c=C)
        raw_fc2 = vflat[:, FCN:2 * FCN].rearrange("p (e r c) -> p e r c", e=E, c=C)
        fc1_b_col = small[:, 2 * C:2 * C + E * HC]
        fc2_b_col = small[:, 2 * C + 32:2 * C + 40]
        g_col, b_col, attn_b_col = (small[:, 2 * C + 40 + i:2 * C + 41 + i] for i in range(3))
        attn_wT, next_wT = small[:, 0:C], small[:, C:2 * C]

        ids_loaded, tables_loaded, w_loaded = sem("ids_loaded"), sem("tables_loaded"), sem("w_loaded")
        small_loaded, fc_loaded = sem("small_loaded"), sem("fc_loaded")
        out_stored = [sem("out_stored_even"), sem("out_stored_odd")]
        zeroed, consts_made = sem("zeroed"), sem("consts_made")
        iota_cast, onehot_made, diag_made = sem("iota_cast"), sem("onehot_made"), sem("diag_made")
        turned, tables_sb, folded_ready, folded_sb = sem("turned"), sem("tables_sb"), sem("folded_ready"), sem("folded_sb")
        weights_sb, wv_rest, small_sb = sem("weights_sb"), sem("wv_rest"), sem("small_sb")
        conv_filled, h0_made, residual_made = sem("conv_filled"), sem("h0_made"), sem("residual_made")
        xt_filled, x_rounded, x_rest = sem("xt_filled"), sem("x_rounded"), sem("x_rest")
        v_filled, v_even_sb, v_odd_sb = sem("v_filled"), sem("v_even_sb"), sem("v_odd_sb")
        ln_stats, ln_aggr, ln_std, ln_rstd, ln_out = (sem(n) for n in ("ln_stats", "ln_aggr", "ln_std", "ln_rstd", "ln_out"))
        pads_made = sem("pads_made")
        filled = sem("filled")
        pv_done = sem("pv_done")
        exped = sem("exped")
        rounded = sem("rounded")
        split = sem("split")
        maxed = sem("maxed")
        rows_made = sem("rows_made")
        summed = [sem("summed_a"), sem("summed_b")]
        den_copied = sem("den_copied")
        o_copied = sem("o_copied")
        inverted = sem("inverted")
        normalised = sem("normalised")
        w_staged = sem("w_staged")
        v_staged = sem("v_staged")
        wo_filled, h1_made, nt_filled, normT_made = sem("wo_filled"), sem("h1_made"), sem("nt_filled"), sem("normT_made")
        xa_filled, xa_made = sem("xa_filled"), sem("xa_made")
        fct_filled, fct_even_sb, fct_odd_sb = sem("fct_filled"), sem("fct_even_sb"), sem("fct_odd_sb")
        hid_filled, hid_made, y_filled, y_made = sem("hid_filled"), sem("hid_made"), sem("y_filled"), sem("y_made")
        z_filled, z_biased, z_made, out_made = sem("z_filled"), sem("z_biased"), sem("z_made"), sem("out_made")

        def release(item, s, v):
            kind = item[0]
            if kind == "exp":
                return exped, s * 2 * KCH + (2 * item[1] + item[2] + 1)
            if kind in "qk":
                return split, v * 4 + (2 * item[1] + (1 if kind == "q" else 2))
            if kind == "max":
                return maxed, v * 2 * KCH + (KCH * item[1] + item[2] + 1)
            if kind == "row":
                return rows_made, v * 2 + (item[1] + 1)
            return den_copied, s + 1

        out_d = out.rearrange("b (e p) c -> e p b c", p=CHUNK)
        block = ctx.enter_context(nc.Block())

        @block.sync
        def _(sp):
            for b in range(B):
                sp.dma_start(ids[:, b * S:(b + 1) * S], x[b:b + 1, :].partition_broadcast(VOCAB)
                             .rearrange("p a n -> p (a n)")).then_inc(ids_loaded, 16)
            sp.dma_start(raw_w[:, 2], wv.rearrange("(r p) c -> p r c", p=128)).then_inc(w_loaded, 16)
            sp.dma_start(raw_wo, wo.rearrange("c (r e) -> c r e", e=128)).then_inc(w_loaded, 16)
            sp.dma_start(raw_small[:, 0, :], attn_w).then_inc(small_loaded, 16)
            sp.dma_start(raw_small[:, 1, :], next_w).then_inc(small_loaded, 16)
            sp.dma_start(raw_bias[0:32, :], fc1_b.rearrange("e (r p) -> (e r) p", p=128)).then_inc(small_loaded, 16)
            sp.dma_start(raw_bias[32:40, :], fc2_b).then_inc(small_loaded, 16)
            for i, vec in enumerate((ln_g, ln_b, attn_b)):
                sp.dma_start(raw_bias[40 + i:41 + i, :], vec.rearrange("(a c) -> a c", a=1)).then_inc(small_loaded, 16)
            sp.dma_start(next_b_row[:, :], next_b.rearrange("(a c) -> a c", a=1).partition_broadcast(128)
                         .rearrange("p a c -> p (a c)")).then_inc(small_loaded, 16)
            sp.wait_ge(v_staged, STEPS)
            for e in range(0, E, 2):
                sp.dma_start(raw_fc1[:, e:e + 2], fc1_w[e:e + 2].rearrange("e (r p) c -> p e r c", p=128)).then_inc(fc_loaded, 16)
                sp.dma_start(raw_fc2[:, e:e + 2], fc2_w[e:e + 2].rearrange("e d (r c) -> d e r c", c=C)).then_inc(fc_loaded, 16)
            for e in range(E):
                sp.wait_ge(out_made, e + 1)
                sp.dma_start(out_d[e], out_sb[e % 2][:, :, :]).then_inc(out_stored[e % 2], 16)
            for stored in out_stored:
                sp.wait_ge(stored, 16 * E // 2)

        @block.tensor
        def _(pe):
            pe.wait_ge(consts_made, 1)
            pe.wait_ge(tables_loaded, 32)
            pe.transpose(bank(0)[:, 0:VOCAB], emb_sb[:, :], ident[0:VOCAB, 0:VOCAB])
            pe.wait_ge(diag_made, TAPS)
            for t in range(TAPS):
                last = pe.transpose(bank(0)[:, (t + 1) * C:(t + 2) * C], conv_diag[:, t, :], ident[:, :])
            last.then_inc(turned, 1)
            pe.wait_ge(w_loaded, 64)
            for w in range(3):
                for r in range(PAIRS):
                    last = pe.transpose(bank(1 + w)[:, r * 128:(r + 1) * 128], raw_w[:, w, r, :], ident[:, :])
                last.then_inc(turned, 1)
            for r in range(PAIRS):
                last = pe.transpose(bank(4)[:, r * C:(r + 1) * C], raw_wo[:, r, :], ident[:, :])
            last.then_inc(turned, 1)
            pe.wait_ge(tables_sb, 2)
            pe.matmul(bank(7)[0:VOCAB, 0:TAPS * C], embT[:, :], convT[:, :], start=True, stop=True).then_inc(folded_ready, 1)
            pe.wait_ge(small_loaded, 16 * 8)
            for i in range(2):
                pe.transpose(bank(5)[:, i * C:(i + 1) * C], raw_small[:, i, :], ident[:, :])
            pe.transpose(bank(5)[:, 2 * C:2 * C + 43], raw_bias[:, :], ident[0:43, 0:43]).then_inc(turned, 1)

            def conv(g):
                if g == 0:
                    pe.wait_ge(folded_sb, 1)
                    pe.wait_ge(onehot_made, B + 1)
                    pe.wait_ge(weights_sb, 2)
                if g >= 2:
                    pe.wait_ge(h0_made, g - 1)
                for j in range(GROUP):
                    b, c0 = divmod((g * GROUP + j) * CHUNK, S)
                    for t in range(TAPS):
                        last = pe.matmul(bank(g % 2)[:, j * C:(j + 1) * C], onehot[:, b, c0 + t:c0 + t + CHUNK],
                                         folded[:, t * C:(t + 1) * C], start=(t == 0), stop=(t == TAPS - 1))
                last.then_inc(conv_filled, 1)

            conv(0)
            conv(1)
            for g in range(NG):
                pe.wait_ge(ln_out, GROUP * (g + 1))
                if g == 0:
                    pe.wait_ge(weights_sb, 6)
                    pe.wait_ge(wv_rest, 1)
                    pe.wait_ge(small_sb, 1)
                if g >= 2:
                    pe.wait_ge(x_rest, g - 1)
                for j in range(GROUP):
                    last = pe.transpose(bank(2 + g % 2)[:, j * CHUNK:(j + 1) * CHUNK], x1[:, g * GROUP + j, :], ident[:, :])
                last.then_inc(xt_filled, 1)
                if g + 2 < NG:
                    conv(g + 2)
                pe.wait_ge(x_rest, g + 1)
                for j in range(GROUP):
                    t = g * GROUP + j
                    if t >= 4:
                        pe.wait_ge((v_even_sb, v_odd_sb)[t % 2], (t - 4) // 2 + 1)
                    rows = slice(t * CHUNK, (t + 1) * CHUNK)
                    for i, (xs, ws) in enumerate(((xR, wvR), (xL, wvR), (xR, wvL))):
                        last = pe.matmul(bank(4 + t % 4), xs[:, rows], ws[:, :], start=(i == 0), stop=(i == 2))
                    last.then_inc(v_filled, 1)

            def prep_item(item, slot, p, v, token0):
                kind, h = item[0], item[1]
                if kind in "qk":
                    if kind == "q" and h == 0:
                        pe.wait_ge(w_staged, v * 2 + 2)
                    w = (0 if kind == "q" else 2) + h
                    for half in range(2):
                        cols = bass.ds(token0 + half * BANK, BANK)
                        for i, (ws, xs) in enumerate(((w_stR, xR), (w_stL, xR), (w_stR, xL))):
                            last = pe.matmul(slot[:, half * BANK:(half + 1) * BANK],
                                             ws[:, w].rearrange("c a d -> c (a d)"), xs[:, cols],
                                             start=(i == 0), stop=(i == 2))
                elif kind == "max":
                    qc = item[2]
                    if qc == 0:
                        pe.wait_ge(split, v * 4 + (2 * h + 2))
                    for half in range(2):
                        cols = slice(half * BANK, (half + 1) * BANK)
                        last = pe.matmul(slot[:, cols], q_full[p][h][:, qc * CHUNK:(qc + 1) * CHUNK],
                                         k_round[p][h][:, cols], start=True, stop=True)
                else:
                    pe.wait_ge(maxed, v * 2 * KCH + KCH * (h + 1))
                    last = pe.transpose(slot[0:KCH, 0:CHUNK], maxes[h][:, :], ident[:, :])
                last.then_inc(filled, 1)

            def pe_step(s, p, prepare, s_is_first=False):
                v = s + 1
                token0 = (v // PAIRS) * S if prepare else 0
                plan = list(numbered(False, prepare))
                if s_is_first:
                    earlier = [(i, n, None, 0) for i, n in numbered(True)]
                else:
                    earlier = [(i, n, s - 1, s) for i, n in numbered(False, True) if n is not None]
                emptied = [release(i, es, ev) for i, n, es, ev in earlier[-SLOTS:]]
                for item, n in plan:
                    if n is None:
                        kc = item[1]
                        pe.wait_ge(exped, s * 2 * KCH + (2 * kc + 2))
                        if kc == 0:
                            pe.wait_ge(v_staged, s + 1)
                            if not s_is_first:
                                pe.wait_ge(o_copied, s)
                        for half in range(2):
                            cols = slice(half * BANK, (half + 1) * BANK)
                            for h in range(2):
                                last = pe.matmul(acc_o[h * D:(h + 1) * D, cols], v_st[p][:, kc, h * D:(h + 1) * D],
                                                 probs[h][kc % 2][:, cols], start=(kc == 0), stop=(kc == KCH - 1))
                        last.then_inc(pv_done, 1)
                        continue
                    slot = slots[slot_of(False, n)]
                    pe.wait_ge(*emptied[n])
                    emptied.append(release(item, s, v))
                    if item[0] == "exp":
                        _, kc, h = item
                        if kc == 0:
                            pe.wait_ge(rows_made, s * 2 + (h + 1))
                        keys = slice(kc * CHUNK, (kc + 1) * CHUNK)
                        for i, (ks, qs) in enumerate(((k_round, q_full), (k_rest, q_max))):
                            for half in range(2):
                                cols = slice(half * BANK, (half + 1) * BANK)
                                last = pe.matmul(slot[:, cols], ks[p][h][:, keys], qs[p][h][:, cols],
                                                 start=(i == 0), stop=(i == 1))
                        last.then_inc(filled, 1)
                    elif item[0] == "den":
                        for h in range(2):
                            pe.wait_ge(summed[h], (s + 1) * (KCH - 1))
                        for half in range(2):
                            cols = slice(half * BANK, (half + 1) * BANK)
                            for h in range(2):
                                last = pe.matmul(slot[h * D:(h + 1) * D, cols], ones64[:, :], sums[h][:, cols],
                                                 start=True, stop=True)
                        last.then_inc(filled, 1)
                    else:
                        prep_item(item, slot, 1 - p, v, token0)

            pe.wait_ge(v_even_sb, NCH // 2)
            pe.wait_ge(v_odd_sb, NCH // 2)
            pe.wait_ge(pads_made, 1)
            emptied = []
            for item, n in numbered(True):
                if n >= SLOTS:
                    pe.wait_ge(*emptied[n - SLOTS])
                emptied.append(release(item, 0, 0))
                prep_item(item, slots[slot_of(True, n)], 0, 0, 0)
            pe_step(0, 0, True, s_is_first=True)
            with pe.Fori(1, STEPS - 2, 2) as it:
                pe_step(it, 1, True)
                pe_step(it + 1, 0, True)
            pe_step(STEPS - 1, 1, False)

            def fct(k):
                if k >= 4:
                    pe.wait_ge((fct_even_sb, fct_odd_sb)[k % 2], (k - 4) // 2 + 1)
                pe.wait_ge(fc_loaded, 16 * 2 * E // 2)
                raw = raw_fc1 if k % 2 == 0 else raw_fc2
                for r in range(HC):
                    last = pe.transpose(bank(k % 4)[:, r * C:(r + 1) * C], raw[:, k // 2, r, :], ident[:, :])
                last.then_inc(fct_filled, 1)

            pe.wait_ge(o_copied, STEPS)
            pe.wait_ge(den_copied, STEPS)
            for g in range(NG):
                if g < NG // B:
                    pe.wait_ge(normalised, PAIRS)
                else:
                    if g == NG // B:
                        for k in range(4):
                            fct(k)
                    pe.wait_ge(normalised, STEPS)
                for j in range(GROUP):
                    b, kc = divmod(g * GROUP + j, KCH)
                    for r in range(PAIRS):
                        last = pe.matmul(bank(4 + g)[:, j * C:(j + 1) * C],
                                         attn_out[:, b * PAIRS + r, kc * CHUNK:(kc + 1) * CHUNK], woT[:, r, :],
                                         start=(r == 0), stop=(r == PAIRS - 1))
                last.then_inc(wo_filled, 1)
            for k in range(4, 8):
                fct(k)
            for g in range(NG):
                pe.wait_ge(ln_out, GROUP * (NG + 2 * g + 2))
                for j in range(GROUP):
                    last = pe.transpose(bank(4 + g)[:, j * CHUNK:(j + 1) * CHUNK], normed2[:, g * GROUP + j, :], ident[:, :])
                last.then_inc(nt_filled, 1)
                fct(8 + 2 * g)
                fct(9 + 2 * g)
                pe.wait_ge(normT_made, g + 1)
                pe.matmul(bank(4 + g), attn_wT, normT[g % 2][:, :], start=True, stop=False, skip_group_check=True)
                for j in range(GROUP):
                    last = pe.matmul(bank(4 + g)[:, j * CHUNK:(j + 1) * CHUNK], h1n[:, g * GROUP + j, :], ident[:, :],
                                     start=False, stop=True, skip_group_check=True)
                last.then_inc(xa_filled, 1)

            def hidden(e):
                if e == 0:
                    pe.wait_ge(fct_even_sb, E)
                    pe.wait_ge(fct_odd_sb, E)
                    pe.wait_ge(xa_made, NG)
                if e >= SLOTS:
                    pe.wait_ge(hid_made, HC * (e - SLOTS + 1))
                toks = xaT[:, :].rearrange("c (b n) -> c b n", b=B)[:, :, e * CHUNK:(e + 1) * CHUNK]
                slot = slots[e % SLOTS][:, :].rearrange("p (r b n) -> p r b n", r=HC, b=B)
                for r in range(HC):
                    last = pe.matmul(slot[:, r], fc1T[:, e, r, :], toks, start=True, stop=True)
                last.then_inc(hid_filled, 1)

            def second(e):
                pe.wait_ge(hid_made, HC * (e + 1))
                if e >= 2:
                    pe.wait_ge(z_biased, e - 1)
                for r in range(HC):
                    last = pe.matmul(acc_o[:, (e % 2) * BANK:(e % 2) * BANK + B * CHUNK], fc2T[:, e, r, :],
                                     hidT[e % 2][:, r, :], start=(r == 0), stop=(r == HC - 1))
                last.then_inc(y_filled, 1)

            def third(e):
                pe.wait_ge(y_made, e + 1)
                for b in range(B):
                    o = (e % 2) * BANK + B * CHUNK + b * C
                    last = pe.matmul(acc_o[:, o:o + C], yT[e % 2][:, b * CHUNK:(b + 1) * CHUNK], next_wT,
                                     start=True, stop=True)
                last.then_inc(z_filled, 1)

            for e in range(E + 2):
                if e < E:
                    hidden(e)
                if 1 <= e <= E:
                    second(e - 1)
                if e >= 2:
                    third(e - 2)

        @block.scalar
        def _(act):
            act.dma_start(emb_sb[:, :], emb).then_inc(tables_loaded, 16)
            act.dma_start(conv_sb[:, :, :], conv_w).then_inc(tables_loaded, 16)
            act.dma_start(raw_w[:, 0], wq.rearrange("(r p) c -> p r c", p=128)).then_inc(w_loaded, 16)
            act.dma_start(raw_w[:, 1], wk.rearrange("(r p) c -> p r c", p=128)).then_inc(w_loaded, 16)
            for w in range(2):
                act.wait_ge(turned, 2 + w)
                src = bank(1 + w).rearrange("c (r n) -> c r n", n=128)
                act.copy(wqk[:, :, w, :], src).then_inc(weights_sb, 1)
            act.wait_ge(turned, 4)
            act.copy(wvR[:, :], bank(3)).then_inc(weights_sb, 2)
            act.wait_ge(turned, 5)
            act.copy(woT[:, :, :], bank(4).rearrange("p (r c) -> p r c", c=C)).then_inc(weights_sb, 2)

            def ln_sqrt(n):
                act.wait_ge(ln_aggr, GROUP * (n + 1))
                act.activation(std[:, :], mv[:, :, 1], ACT.Sqrt, bias=eps[:, 0:1]).then_inc(ln_std, 1)

            def relu(g):
                act.wait_ge(conv_filled, g + 1)
                act.activation(h0[:, g * GROUP:(g + 1) * GROUP, :],
                               bank(g % 2).rearrange("p (t c) -> p t c", c=C), ACT.Relu).then_inc(h0_made, 1)

            act.wait_ge(consts_made, 1)
            relu(0)
            relu(1)
            for g in range(NG):
                ln_sqrt(g)
                act.wait_ge(xt_filled, g + 1)
                act.copy(xR[:, g * BANK:(g + 1) * BANK], bank(2 + g % 2)).then_inc(x_rounded, 1)
                if g + 2 < NG:
                    relu(g + 2)
                for j in range(0, GROUP, 2):
                    b, kc = divmod(g * GROUP + j, KCH)
                    act.wait_ge(v_filled, g * GROUP + j + 1)
                    act.copy(v_all[:, b * PAIRS:(b + 1) * PAIRS, kc, :],
                             bank(4 + j).rearrange("p (r d) -> p r d", r=PAIRS)).then_inc(v_even_sb, 1)

            def act_item(item, n, count, slot, p, s, first):
                kind = item[0]
                if kind == "exp":
                    _, kc, h = item
                    act.wait_ge(filled, count)
                    if not (first and kc < 2):
                        act.wait_ge(pv_done, s * KCH + (kc - 1))
                        act.wait_ge(summed[h], s * (KCH - 1) + adds_before_reuse(kc))
                    act.activation(probs[h][kc % 2][:, :], slot[:, :], ACT.Exp, scale=SCALE).then_inc(exped, 1)
                elif kind == "q":
                    h = item[1]
                    act.wait_ge(filled, count)
                    act.copy(q_full[p][h][:, :], slot[:, :]).then_inc(rounded, 1)
                    act.copy(q_max[p][h][0:D, :], slot[0:D, :]).then_inc(rounded, 1)
                elif kind == "k":
                    act.wait_ge(filled, count)
                    act.copy(k_round[p][item[1]][:, :], slot[:, :]).then_inc(rounded, 1)
                elif kind == "den":
                    act.wait_ge(pv_done, s * KCH + KCH)
                    if not first:
                        act.wait_ge(normalised, s)
                    act.copy(o_sb[:, :], acc_o[:, :]).then_inc(o_copied, 1)
                    act.wait_ge(filled, count)
                    act.copy(den_sb[:, :], slot[:, :]).then_inc(den_copied, 1)

            def act_step(s, p, prepare, first=False):
                for item, n in numbered(False, prepare):
                    if n is not None:
                        act_item(item, n, item_count(s, n), slots[slot_of(False, n)],
                                 p if item[0] == "exp" else 1 - p, s, first)

            act.wait_ge(pads_made, 1)
            for item, n in numbered(True):
                act_item(item, n, item_count(None, n), slots[slot_of(True, n)], 0, 0, True)
            act_step(0, 0, True, first=True)
            with act.Fori(1, STEPS - 2, 2) as it:
                act_step(it, 1, True)
                act_step(it + 1, 0, True)
            act_step(STEPS - 1, 1, False)

            def fct_copy(k):
                act.wait_ge(fct_filled, k + 1)
                act.copy(fc1T[:, k // 2, :, :], bank(k % 4).rearrange("p (r c) -> p r c", c=C)).then_inc(fct_even_sb, 1)

            def norm_t(g):
                act.wait_ge(nt_filled, g + 1)
                if g >= 2:
                    act.wait_ge(xa_filled, g - 1)
                act.activation(normT[g % 2][:, :], bank(4 + g), ACT.Identity, bias=b_col, scale=g_col).then_inc(normT_made, 1)

            def xa_copy(g):
                act.wait_ge(xa_filled, g + 1)
                act.activation(xaT[:, g * BANK:(g + 1) * BANK], bank(4 + g), ACT.Identity, bias=attn_b_col).then_inc(xa_made, 1)

            act.wait_ge(o_copied, STEPS)
            for what, i in (("ln", 0), ("fct", 0), ("fct", 2), ("ln", 1), ("fct", 4), ("fct", 6), ("nt", 0),
                            ("ln", 2), ("fct", 8), ("xa", 0), ("nt", 1), ("fct", 10),
                            ("ln", 3), ("xa", 1), ("nt", 2), ("fct", 12), ("xa", 2), ("nt", 3), ("fct", 14), ("xa", 3)):
                if what == "ln":
                    ln_sqrt(NG + 2 * i)
                    ln_sqrt(NG + 2 * i + 1)
                elif what == "fct":
                    fct_copy(i)
                elif what == "nt":
                    norm_t(i)
                else:
                    xa_copy(i)

            for e in range(E + 2):
                if e < E:
                    act.wait_ge(hid_filled, e + 1)
                    if e >= 2:
                        act.wait_ge(y_filled, e - 1)
                    slot = slots[e % SLOTS][:, :].rearrange("p (r n) -> p r n", r=HC)
                    for r in range(HC):
                        act.activation(hidT[e % 2][:, r, :], slot[:, r, :], ACT.Gelu,
                                       bias=fc1_b_col[:, e * HC + r:e * HC + r + 1]).then_inc(hid_made, 1)
                if e >= 2:
                    act.wait_ge(z_biased, e - 1)
                    if e >= 4:
                        act.wait_ge(out_made, e - 3)
                    act.activation(z_act[e % 2][:, :, :], z_pre[e % 2][:, :, :], ACT.Gelu).then_inc(z_made, 1)

        @block.vector
        def _(dve):
            dve.wait_ge(consts_made, 1)
            dve.tensor_copy(iota_f[:, :], iota_i[:, :]).then_inc(iota_cast, 1)
            dve.memset(onehot[:, :, 0:1], 0.0).then_inc(onehot_made, 1)
            dve.wait_ge(tables_loaded, 32)
            for t in range(TAPS):
                dve.tensor_tensor(conv_diag[:, t, :].rearrange("o (g i) -> o g i", i=4),
                                  conv_sb[:, :, t].unsqueeze(1).broadcast_to([C, 32, 4]),
                                  group_mask[:, :].unsqueeze(2).broadcast_to([C, 32, 4]), ALU.mult).then_inc(diag_made, 1)
            dve.wait_ge(iota_cast, 1)
            dve.wait_ge(ids_loaded, 16 * B)
            for b in range(B):
                dve.tensor_scalar(onehot[:, b, 1:S + 1], ids[:, b * S:(b + 1) * S], float(VOCAB - 1),
                                  iota_f[0:VOCAB, 0:1], ALU.min, ALU.is_equal).then_inc(onehot_made, 1)
            dve.wait_ge(turned, 1)
            dve.tensor_copy(embT[:, :], bank(0)[:, 0:VOCAB]).then_inc(tables_sb, 1)
            dve.tensor_copy(convT[:, :], bank(0)[:, C:(TAPS + 1) * C]).then_inc(tables_sb, 1)
            dve.wait_ge(folded_ready, 1)
            dve.tensor_copy(folded[:, :], bank(7)[0:VOCAB, 0:TAPS * C]).then_inc(folded_sb, 1)
            dve.wait_ge(weights_sb, 4)
            dve.tensor_tensor(wvL[:, :], bank(3), wvR[:, :].bitcast(F32), ALU.subtract).then_inc(wv_rest, 1)
            dve.wait_ge(turned, 6)
            dve.tensor_copy(small[:, :], bank(5)[:, 0:2 * C + 43]).then_inc(small_sb, 1)

            def layernorm(n, src, dst):
                if n:
                    dve.wait_ge(ln_out, GROUP * n)
                for j in range(GROUP):
                    dve.bn_stats(stats[:, j, :], src[:, j, :]).then_inc(ln_stats, 1)
                for j in range(GROUP):
                    dve.wait_ge(ln_stats, GROUP * n + j + 1)
                    dve.bn_aggr(mv[:, j, :], stats[:, j, :]).then_inc(ln_aggr, 1)
                dve.wait_ge(ln_std, n + 1)
                dve.reciprocal(rstd[:, :], std[:, :]).then_inc(ln_rstd, 1)
                dve.wait_ge(ln_rstd, n + 1)
                for j in range(GROUP):
                    dve.tensor_scalar(dst[:, j, :], src[:, j, :], mv[:, j, 0:1], rstd[:, j:j + 1],
                                      ALU.subtract, ALU.mult).then_inc(ln_out, 1)

            for g in range(NG):
                own = slice(g * GROUP, (g + 1) * GROUP)
                dve.wait_ge(h0_made, g + 1)
                layernorm(g, h0[:, own, :], x1[:, own, :])
                dve.wait_ge(x_rounded, g + 1)
                dve.tensor_tensor(xL[:, g * BANK:(g + 1) * BANK], bank(2 + g % 2),
                                  xR[:, g * BANK:(g + 1) * BANK].bitcast(F32), ALU.subtract).then_inc(x_rest, 1)
                for j in range(1, GROUP, 2):
                    b, kc = divmod(g * GROUP + j, KCH)
                    dve.wait_ge(v_filled, g * GROUP + j + 1)
                    dve.tensor_copy(v_all[:, b * PAIRS:(b + 1) * PAIRS, kc, :],
                                    bank(4 + j).rearrange("p (r d) -> p r d", r=PAIRS)).then_inc(v_odd_sb, 1)

            def stage_w(v):
                src = wqk[:, v % PAIRS, :, :].rearrange("c w (h d) -> c (w h) d", d=D).unsqueeze(2).broadcast_to([C, 4, 2, D])
                dve.tensor_copy(w_stR[:, :, :, :], src).then_inc(w_staged, 1)
                dve.wait_ge(w_staged, v * 2 + 1)
                dve.tensor_tensor(w_stL[:, :, :, :], src, w_stR[:, :, :, :].bitcast(F32), ALU.subtract).then_inc(w_staged, 1)

            def dve_item(item, count, slot, p, s, v, first):
                kind = item[0]
                if kind == "exp":
                    _, kc, h = item
                    if h == 1 and kc >= 1:
                        dve.wait_ge(exped, s * 2 * KCH + (2 * kc + 1))
                        if kc == 1 and not first:
                            dve.wait_ge(den_copied, s)
                        if kc > 1:
                            dve.wait_ge(summed[0], s * (KCH - 1) + (kc - 1))
                        before = probs[0][0] if kc == 1 else sums[0]
                        dve.tensor_tensor(sums[0][:, :], before[:, :], probs[0][kc % 2][:, :], ALU.add).then_inc(summed[0], 1)
                elif kind == "q":
                    h = item[1]
                    dve.wait_ge(rounded, v * 6 + (3 * h + 2))
                    dve.tensor_tensor(q_full[p][h][D:128, :], slot[D:128, :], q_full[p][h][D:128, :].bitcast(F32),
                                      ALU.subtract).then_inc(split, 1)
                elif kind == "k":
                    h = item[1]
                    dve.wait_ge(rounded, v * 6 + (3 * h + 3))
                    dve.tensor_tensor(k_rest[p][h][0:D, :], slot[0:D, :], k_round[p][h][0:D, :].bitcast(F32),
                                      ALU.subtract).then_inc(split, 1)
                elif kind == "max":
                    _, h, qc = item
                    dve.wait_ge(filled, count)
                    dve.reduce_max(maxes[h][:, qc:qc + 1], slot[:, :], AX.X).then_inc(maxed, 1)
                elif kind == "row":
                    h = item[1]
                    dve.wait_ge(filled, count)
                    dve.tensor_tensor(q_max[p][h][D:D + KCH, :].rearrange("c (a n) -> c a n", a=KCH),
                                      slot[0:KCH, 0:CHUNK].unsqueeze(1).broadcast_to([KCH, KCH, CHUNK]),
                                      chunk_mask[:, :, :], ALU.mult).then_inc(rows_made, 1)

            def invert(s, i):
                dve.wait_ge(den_copied, s + 1)
                cols = slice(i * S // QUARTERS, (i + 1) * S // QUARTERS)
                dve.reciprocal(den_sb[:, cols], den_sb[:, cols]).then_inc(inverted, 1)

            def dve_step(s, p, prepare, first=False):
                quarters = list(range(0 if first else QUARTERS))
                for item, n in numbered(False, prepare):
                    if quarters and (item[0] in "qk" or not prepare and item[0] == "exp" and item[2]):
                        invert(s - 1, quarters.pop(0))
                    if n is not None:
                        dve_item(item, item_count(s, n), slots[slot_of(False, n)], 1 - p, s, s + 1, first)
                    if item == ("max", 0, 2):
                        stage_w(s + 2)

            dve.wait_ge(pads_made, 1)
            stage_w(0)
            for item, n in numbered(True):
                dve_item(item, item_count(None, n), slots[slot_of(True, n)], 0, 0, 0, True)
                if item == ("max", 0, 2):
                    stage_w(1)
            dve_step(0, 0, True, first=True)
            with dve.Fori(1, STEPS - 2, 2) as it:
                dve_step(it, 1, True)
                dve_step(it + 1, 0, True)
            dve_step(STEPS - 1, 1, False)
            for i in range(QUARTERS):
                invert(STEPS - 1, i)

            def fct_copy(k):
                dve.wait_ge(fct_filled, k + 1)
                dve.tensor_copy(fc2T[:, k // 2, :, :], bank(k % 4).rearrange("p (r c) -> p r c", c=C)).then_inc(fct_odd_sb, 1)

            for g in range(NG):
                own = slice(g * GROUP, (g + 1) * GROUP)
                dve.wait_ge(wo_filled, g + 1)
                dve.wait_ge(residual_made, NG)
                dve.tensor_tensor(residual[:, own, :], bank(4 + g).rearrange("p (t c) -> p t c", c=C),
                                  residual[:, own, :], ALU.add).then_inc(h1_made, 1)
                dve.wait_ge(h1_made, g + 1)
                layernorm(NG + 2 * g, residual[:, own, :], h1n[:, own, :])
                layernorm(NG + 2 * g + 1, h1n[:, own, :], normed2[:, own, :])
                for k in (4 * g + 1, 4 * g + 3):
                    fct_copy(k)

            for e in range(E + 1):
                if e < E:
                    dve.wait_ge(y_filled, e + 1)
                    dve.tensor_scalar(yT[e % 2][:, :], acc_o[:, (e % 2) * BANK:(e % 2) * BANK + B * CHUNK],
                                      fc2_b_col[:, e:e + 1], None, ALU.add).then_inc(y_made, 1)
                if e >= 1:
                    i = (e - 1) % 2
                    dve.wait_ge(z_filled, e)
                    if e >= 3:
                        dve.wait_ge(z_made, e - 2)
                    dve.tensor_tensor(z_pre[i][:, :, :],
                                      acc_o[:, i * BANK + B * CHUNK:(i + 1) * BANK].rearrange("p (b c) -> p b c", b=B),
                                      next_b_row[:, :].unsqueeze(1).broadcast_to([128, B, C]), ALU.add).then_inc(z_biased, 1)

        @block.gpsimd
        def _(pool):
            pool.memset(ident[:, :], 0.0).then_inc(zeroed, 1)
            pool.memset(chunk_mask[:, :, :], 0.0).then_inc(zeroed, 1)
            pool.memset(group_mask[:, :], 1.0).then_inc(zeroed, 1)
            pool.memset(ones64[:, :], 1.0)
            pool.memset(eps[:, :], EPS)
            pool.iota(iota_i[:, :], pattern=[[0, 1]], base=0, channel_multiplier=1)
            pool.wait_ge(zeroed, 3)
            pool.affine_select(out=group_mask[:, :], in_=group_mask[:, :], compare_op=ALU.is_ge, fill=0.0, base=0,
                               pattern=[[-4, 32]], channel_multiplier=1).then_inc(zeroed, 1)
            pool.wait_ge(zeroed, 4)
            pool.affine_select(out=group_mask[:, :], in_=group_mask[:, :], compare_op=ALU.is_ge, fill=0.0, base=3,
                               pattern=[[4, 32]], channel_multiplier=-1)
            pool.affine_select(out=ident[:, :], in_=ident[:, :], compare_op=ALU.not_equal, fill=1.0, base=0,
                               pattern=[[-1, 128]], channel_multiplier=1).then_inc(consts_made, 1)
            pool.affine_select(out=chunk_mask[:, :, :], in_=chunk_mask[:, :, :], compare_op=ALU.not_equal, fill=-1.0, base=0,
                               pattern=[[-1, KCH], [0, CHUNK]], channel_multiplier=1)
            for p in range(2):
                for h in range(2):
                    pool.memset(q_max[p][h][:, :].bitcast(F32), 0.0)
                    last = pool.memset(k_rest[p][h][:, :].bitcast(F32), 1.0)
            last.then_inc(pads_made, 1)

            def stage_v(v, p):
                pool.tensor_copy(v_st[p][:, :, :], v_all[:, v, :, :]).then_inc(v_staged, 1)

            for g in range(NG):
                own = slice(g * GROUP, (g + 1) * GROUP)
                pool.wait_ge(ln_out, GROUP * (g + 1))
                pool.wait_ge(onehot_made, B + 1)
                pool.tensor_tensor(residual[:, own, :], h0[:, own, :], x1[:, own, :], ALU.add).then_inc(residual_made, 1)
            pool.wait_ge(v_even_sb, NCH // 2)
            pool.wait_ge(v_odd_sb, NCH // 2)
            stage_v(0, 0)

            def normalise(s):
                pool.wait_ge(inverted, s * QUARTERS + QUARTERS)
                pool.tensor_tensor(attn_out[:, s, :], o_sb[:, :], den_sb[:, :], ALU.mult).then_inc(normalised, 1)

            def pool_step(s, p, prepare, first=False):
                for kc in range(1, KCH):
                    if kc == 3 and not first:
                        normalise(s - 1)
                    pool.wait_ge(exped, s * 2 * KCH + (2 * kc + 2))
                    if kc == 1 and not first:
                        pool.wait_ge(den_copied, s)
                    if kc > 1:
                        pool.wait_ge(summed[1], s * (KCH - 1) + (kc - 1))
                    before = probs[1][0] if kc == 1 else sums[1]
                    pool.tensor_tensor(sums[1][:, :], before[:, :], probs[1][kc % 2][:, :], ALU.add).then_inc(summed[1], 1)
                    if prepare and kc == 1:
                        if not first:
                            pool.wait_ge(pv_done, s * KCH)
                        stage_v(s + 1, 1 - p)

            pool_step(0, 0, True, first=True)
            with pool.Fori(1, STEPS - 2, 2) as it:
                pool_step(it, 1, True)
                pool_step(it + 1, 0, True)
            pool_step(STEPS - 1, 1, False)

            normalise(STEPS - 1)

            h1 = residual[:, :, :].rearrange("p (b e) c -> p b e c", b=B)
            for e in range(E):
                pool.wait_ge(z_made, e + 1)
                if e >= 2:
                    pool.wait_ge(out_stored[e % 2], 16 * (e // 2))
                pool.tensor_tensor(out_sb[e % 2][:, :, :], z_act[e % 2][:, :, :], h1[:, :, e, :], ALU.add).then_inc(out_made, 1)


_INS = ["x", "L0_tok_emb_table", "L0_tok_conv_w", "L0_attn_Wq", "L0_attn_Wk", "L0_attn_Wv", "L0_attn_Wo",
        "L0_ffn_ln_g", "L0_ffn_ln_b", "L0_ffn_attn_w", "L0_ffn_attn_b", "L0_ffn_fc1_w", "L0_ffn_fc1_b",
        "L0_ffn_fc2_w", "L0_ffn_fc2_b", "L0_ffn_next_w", "L0_ffn_next_b"]
_OUT = ((2, 1024, 128), "float32")


def kernel(**inputs):
    import numpy as np
    import concourse.bacc as bacc
    from concourse.bass_utils import run_bass_kernel_spmd

    nc = bacc.Bacc("TRN2", target_bir_lowering=False, num_devices=1)
    arrays, args = {}, []
    for name in _INS:
        a = np.ascontiguousarray(inputs[name])
        arrays[f"in_{name}"] = a
        args.append(nc.dram_tensor(f"in_{name}", a.shape, mybir.dt.from_np(a.dtype), kind="ExternalInput").ap())
    args.append(nc.dram_tensor("out_h", _OUT[0], mybir.dt.from_np(np.dtype(_OUT[1])), kind="ExternalOutput").ap())
    build(nc, *args)
    r = run_bass_kernel_spmd(nc, [arrays], core_ids=[0])
    return r.results[0]["out_h"]
```

```python
from contextlib import ExitStack

import concourse.bass as bass
from concourse import mybir

F32 = mybir.dt.float32
F32R = mybir.dt.float32r
I32 = mybir.dt.int32
ALU = mybir.AluOpType
ACT = mybir.ActivationFunctionType
AX = mybir.AxisListType

C = 128
B, S = 2, 1024
HEADS, D = 8, 64
PAIRS = HEADS // 2
STEPS = B * PAIRS
CHUNK = 128
NCH = B * S // CHUNK
KCH = S // CHUNK
GROUP = 4
NG = NCH // GROUP
E, HID = 8, 512
HC = HID // 128
TAPS = 2
EPS = 1e-5
SCALE = float(D) ** -0.5
BANK = 512
SLOTS = 3
CONV_BANK = (0, 1, 6, 7)
POOL_ADDS = 3


MAXES = [("max", h, qc) for h in range(2) for qc in range(KCH)]
MAXES_IN = (0, 2, 3, 3, 3, 2, 2, 1)
assert sum(MAXES_IN) == len(MAXES)

PROLOGUE = ([(("k",), -2), (("q",), -2)] + [(item, -1) for item in MAXES]
            + [(("rows",), -1), (("k",), -1), (("q",), -1)])


def step_order(prepare):
    order = []
    for kc in range(KCH):
        at = sum(MAXES_IN[:kc])
        extra = MAXES[at:at + MAXES_IN[kc]] if prepare else []
        pv = [("pv", kc - 1, half) for half in range(2 if kc else 0)]
        order += [("exp", kc, 0)] + extra[:1] + [("exp", kc, 1)] + pv[:1] + extra[1:] + pv[1:]
    if prepare:
        return order + [("k",), ("rows",), ("q",), ("pv", KCH - 1, 0), ("pv", KCH - 1, 1), ("den",)]
    return order + [("pv", KCH - 1, 0), ("pv", KCH - 1, 1), ("den",)]


ITEMS = len([i for i in step_order(True) if i[0] != "pv"])
assert ITEMS % SLOTS == 0


def numbered(prepare=True):
    n = 0
    for item in step_order(prepare):
        if item[0] == "pv":
            yield item, None
        else:
            yield item, n
            n += 1


def item_count(s, n):
    return s * ITEMS + (len(PROLOGUE) + n + 1)


def slot_of(n):
    return (len(PROLOGUE) + n) % SLOTS


def target(item, s):
    return s + {"q": 2, "k": 2, "max": 1, "rows": 1}.get(item[0], 0)


def parity(item, p):
    return 1 - p if item[0] in ("max", "rows") else p


def adds_before_reuse(kc):
    return kc - 1 if kc < 2 else max(kc - 2, 1)


def build(nc, x, emb, conv_w, wq, wk, wv, wo, ln_g, ln_b, attn_w, attn_b,
          fc1_w, fc1_b, fc2_w, fc2_b, next_w, next_b, out):
    VOCAB = emb.shape[0]
    with ExitStack() as ctx:
        def sem(name):
            return ctx.enter_context(nc.semaphore(name))

        def sb(name, shape, dt=F32, scope=ctx):
            return scope.enter_context(nc.sbuf_tensor(name, shape, dt))

        slots = [ctx.enter_context(nc.psum_tensor(f"slot{i}", [128, 2 * BANK], F32)) for i in range(SLOTS)]
        acc_o = ctx.enter_context(nc.psum_tensor("acc_o", [128, 2 * BANK], F32))

        def bank(k):
            t = slots[k // 2] if k < 2 * SLOTS else acc_o
            return t[:, (k % 2) * BANK:(k % 2 + 1) * BANK]

        ident = sb("ident", [128, 128])
        ones32 = sb("ones32", [128, 32])
        iota_i = sb("iota_i", [128, 1], I32)
        iota_f = sb("iota_f", [128, 1])
        eps = sb("eps", [128, 1])
        group_mask = sb("group_mask", [128, 32])
        woT = sb("woT", [128, PAIRS, C])
        small = sb("small", [128, 2 * C + 43])
        next_b_row = sb("next_b_row", [128, C])
        stats = sb("stats", [128, KCH, 6])
        mv = sb("mv", [128, KCH, 2])
        std = sb("std", [128, KCH])
        rstd = sb("rstd", [128, KCH])
        residual = sb("residual", [128, NCH, C])
        attn_out = sb("attn_out", [128, STEPS, S])
        v_all = sb("v_all", [128, STEPS, KCH, 2 * D])

        with ExitStack() as front:
            emb_sb = sb("emb_sb", [VOCAB, C], F32, front)
            conv_sb = sb("conv_sb", [C, 4, TAPS], F32, front)
            conv_diag = sb("conv_diag", [C, TAPS, C], F32, front)
            embT = sb("embT", [C, VOCAB], F32, front)
            convT = sb("convT", [C, TAPS * C], F32, front)
            folded = sb("folded", [VOCAB, TAPS * C], F32, front)
            wvR = sb("wvR", [C, HEADS * D], F32R, front)
            wvL = sb("wvL", [C, HEADS * D], F32R, front)
            raw_small = sb("raw_small", [128, 2, C], F32, front)
            raw_bias = sb("raw_bias", [43, C], F32, front)
        with ExitStack() as att:
            sums = [sb(f"sums{h}", [128, S], F32, att) for h in range(2)]
            den_sb = sb("den_sb", [128, BANK], F32, att)
            den_flat = sb("den_flat", [128, 2 * S // 128], F32, att)
            inv_flat = sb("inv_flat", [128, 2 * S // 128], F32, att)
            inv_sb = sb("inv_sb", [128, S], F32, att)
            o_sb = sb("o_sb", [128, S], F32, att)
            wqk = sb("wqk", [C, PAIRS, 2, 2 * D], F32, att)
            xR = sb("xR", [C, B * S], F32R, att)
            xL = sb("xL", [C, B * S], F32R, att)
            w_stR = sb("w_stR", [C, 2, 2 * D], F32R, att)
            w_stL = sb("w_stL", [C, 2, 2 * D], F32R, att)
            q_full = [[sb(f"q_full{p}{h}", [128, S], F32R, att) for h in range(2)] for p in range(2)]
            q_max = [[sb(f"q_max{p}{h}", [128, S], F32R, att) for h in range(2)] for p in range(2)]
            k_round = [[sb(f"k_round{p}{h}", [128, S], F32R, att) for h in range(2)] for p in range(2)]
            k_rest = [[sb(f"k_rest{p}{h}", [128, S], F32R, att) for h in range(2)] for p in range(2)]
            v_st = [sb(f"v_st{p}", [128, KCH, 2 * D], F32, att) for p in range(2)]
            probs = [[sb(f"probs{h}{i}", [128, S], F32, att) for i in range(2)] for h in range(2)]
            maxes = [sb(f"maxes{h}", [128, KCH], F32, att) for h in range(2)]
            neg_max = sb("neg_max", [KCH, 2, CHUNK], F32R, att)
        fc1T = sb("fc1T", [128, E, HC, C])
        fc2T = sb("fc2T", [128, E, HC, C])
        normed2 = sb("normed2", [128, NCH, C])
        h1n = sb("h1n", [128, NCH, C])
        normT = [sb(f"normT{i}", [128, BANK]) for i in range(2)]
        xaT = sb("xaT", [C, B * S])
        hidT = [sb(f"hidT{i}", [128, HC, B * CHUNK]) for i in range(2)]
        yT = [sb(f"yT{i}", [C, B * CHUNK]) for i in range(2)]
        z_pre = [sb(f"z_pre{i}", [128, B, C]) for i in range(2)]
        z_act = [sb(f"z_act{i}", [128, B, C]) for i in range(2)]
        out_sb = [sb(f"out_sb{i}", [128, B, C]) for i in range(2)]

        flat = attn_out[:, :, :].rearrange("p s n -> p (s n)")
        h0 = flat[:, 0:NCH * C].rearrange("p (t c) -> p t c", c=C)
        x1 = flat[:, NCH * C:2 * NCH * C].rearrange("p (t c) -> p t c", c=C)
        PAD = 2 * NCH * C
        onehot = flat[0:VOCAB, PAD:PAD + B * (S + 1)].rearrange("p (b n) -> p b n", b=B)
        ids = residual[0:VOCAB, :, :].bitcast(I32).rearrange("p t c -> p (t c)")
        vflat = v_all[:, :, :, :].rearrange("p s k d -> p (s k d)")
        raw_w = vflat[:, 0:3 * PAIRS * C].rearrange("p (w r c) -> p w r c", w=3, c=C)
        raw_wo = vflat[:, 3 * PAIRS * C:4 * PAIRS * C].rearrange("p (r c) -> p r c", c=C)
        FCN = E * HC * C
        raw_fc1 = vflat[:, 0:FCN].rearrange("p (e r c) -> p e r c", e=E, c=C)
        raw_fc2 = vflat[:, FCN:2 * FCN].rearrange("p (e r c) -> p e r c", e=E, c=C)
        fc1_b_col = small[:, 2 * C:2 * C + E * HC]
        fc2_b_col = small[:, 2 * C + 32:2 * C + 40]
        g_col, b_col, attn_b_col = (small[:, 2 * C + 40 + i:2 * C + 41 + i] for i in range(3))
        attn_wT, next_wT = small[:, 0:C], small[:, C:2 * C]

        ids_loaded, tables_loaded, w_loaded = sem("ids_loaded"), sem("tables_loaded"), sem("w_loaded")
        small_loaded, fc_loaded = sem("small_loaded"), sem("fc_loaded")
        out_stored = [sem("out_stored_even"), sem("out_stored_odd")]
        zeroed, consts_made = sem("zeroed"), sem("consts_made")
        iota_cast, onehot_made, diag_made = sem("iota_cast"), sem("onehot_made"), sem("diag_made")
        turned, tables_sb, folded_ready, folded_sb = sem("turned"), sem("tables_sb"), sem("folded_ready"), sem("folded_sb")
        weights_sb, wv_rest, small_sb = sem("weights_sb"), sem("wv_rest"), sem("small_sb")
        conv_filled, h0_made, residual_made = sem("conv_filled"), sem("h0_made"), sem("residual_made")
        xt_filled, x_rounded, x_rest = sem("xt_filled"), sem("x_rounded"), sem("x_rest")
        v_filled, v_sb = sem("v_filled"), sem("v_sb")
        x_stats, x_aggr, x_std, x_rstd, x_normed = (sem(n) for n in ("x_stats", "x_aggr", "x_std", "x_rstd", "x_normed"))
        pads_made = sem("pads_made")
        filled = sem("filled")
        pv_done = sem("pv_done")
        exped = sem("exped")
        rounded = sem("rounded")
        k_doubled = sem("k_doubled")
        q_doubled = [sem("q_doubled_even"), sem("q_doubled_odd")]
        split = sem("split")
        maxed = sem("maxed")
        rows_made = sem("rows_made")
        rows_loaded = sem("rows_loaded")
        summed = [sem("summed_a"), sem("summed_b")]
        den_copied = sem("den_copied")
        o_copied = sem("o_copied")
        den_spread = sem("den_spread")
        inverted = sem("inverted")
        inv_stored = sem("inv_stored")
        inv_loaded = sem("inv_loaded")
        normalised = sem("normalised")
        w_staged = sem("w_staged")
        v_staged = sem("v_staged")
        ln_stats, ln_aggr, ln_std, ln_rstd, ln_out = (sem(n) for n in ("ln_stats", "ln_aggr", "ln_std", "ln_rstd", "ln_out"))
        wo_filled, h1_made, nt_filled, normT_made = sem("wo_filled"), sem("h1_made"), sem("nt_filled"), sem("normT_made")
        xa_filled, xa_made = sem("xa_filled"), sem("xa_made")
        fct_filled, fct_even_sb, fct_odd_sb = sem("fct_filled"), sem("fct_even_sb"), sem("fct_odd_sb")
        hid_filled, hid_made, y_filled, y_made = sem("hid_filled"), sem("hid_made"), sem("y_filled"), sem("y_made")
        z_filled, z_biased, z_made, out_made = sem("z_filled"), sem("z_biased"), sem("z_made"), sem("out_made")

        def release(item, s):
            kind, v = item[0], target(item, s)
            if kind == "exp":
                return exped, s * 2 * KCH + (2 * item[1] + item[2] + 1)
            if kind in "qk":
                return split, v * 4 + (2 if kind == "k" else 4)
            if kind == "max":
                return maxed, v * 2 * KCH + (KCH * item[1] + item[2] + 1)
            if kind == "rows":
                return rows_made, v + 1
            return den_copied, s + 1

        inv_dram = nc.dram_tensor("inv_scratch", [128, 2 * S // 128], F32, kind="Internal").ap()
        out_d = out.rearrange("b (e p) c -> e p b c", p=CHUNK)
        block = ctx.enter_context(nc.Block())

        @block.sync
        def _(sp):
            for b in range(B):
                sp.dma_start(ids[:, b * S:(b + 1) * S], x[b:b + 1, :].partition_broadcast(VOCAB)
                             .rearrange("p a n -> p (a n)")).then_inc(ids_loaded, 16)
            sp.dma_start(raw_w[:, 2], wv.rearrange("(r p) c -> p r c", p=128)).then_inc(w_loaded, 16)
            sp.dma_start(raw_wo, wo.rearrange("c (r e) -> c r e", e=128)).then_inc(w_loaded, 16)
            sp.dma_start(raw_small[:, 0, :], attn_w).then_inc(small_loaded, 16)
            sp.dma_start(raw_small[:, 1, :], next_w).then_inc(small_loaded, 16)
            sp.dma_start(raw_bias[0:32, :], fc1_b.rearrange("e (r p) -> (e r) p", p=128)).then_inc(small_loaded, 16)
            sp.dma_start(raw_bias[32:40, :], fc2_b).then_inc(small_loaded, 16)
            for i, vec in enumerate((ln_g, ln_b, attn_b)):
                sp.dma_start(raw_bias[40 + i:41 + i, :], vec.rearrange("(a c) -> a c", a=1)).then_inc(small_loaded, 16)
            sp.dma_start(next_b_row[:, :], next_b.rearrange("(a c) -> a c", a=1).partition_broadcast(128)
                         .rearrange("p a c -> p (a c)")).then_inc(small_loaded, 16)

            def spread(s):
                sp.wait_ge(den_copied, s + 1)
                sp.dma_start(den_flat[:, :], den_sb[0:128:32, :]).then_inc(den_spread, 16)
                sp.wait_ge(inverted, s + 1)
                sp.dma_start(inv_dram[:, :], inv_flat[:, :]).then_inc(inv_stored, 16)
                sp.wait_ge(inv_stored, s * 16 + 16)
                for h in range(2):
                    sp.dma_start(inv_sb[h * D:(h + 1) * D, :],
                                 inv_dram[h * 64:(h + 1) * 64, :].rearrange("(a p) n -> a (p n)", a=1)
                                 .partition_broadcast(D).rearrange("p a n -> p (a n)")).then_inc(inv_loaded, 16)

            def double(p, v):
                sp.wait_ge(rounded, v * 4 + 2)
                for h in range(2):
                    sp.dma_start(k_round[p][h][D:128, :].bitcast(F32), k_round[p][h][0:D, :].bitcast(F32)).then_inc(k_doubled, 16)
                sp.wait_ge(rounded, v * 4 + 4)
                for h in range(2):
                    sp.dma_start(q_max[p][h][0:D, :].bitcast(F32), q_full[p][h][0:D, :].bitcast(F32)).then_inc(q_doubled[p], 16)

            def max_rows(p, v):
                sp.wait_ge(rows_made, v + 1)
                for h in range(2):
                    sp.dma_start(q_max[p][h][D:D + 1, :].bitcast(F32).rearrange("a (c n) -> a c n", c=KCH),
                                 neg_max[:, h, :].bitcast(F32)).then_inc(rows_loaded, 16)

            def sp_step(s, p):
                max_rows(1 - p, s + 1)
                double(p, s + 2)
                spread(s)

            sp.wait_ge(pads_made, 1)
            double(0, 0)
            max_rows(0, 0)
            double(1, 1)
            sp_step(0, 0)
            with sp.Fori(1, STEPS - 2, 2) as it:
                sp_step(it, 1)
                sp_step(it + 1, 0)
            sp.wait_ge(v_staged, STEPS)
            for e in range(0, E, 2):
                sp.dma_start(raw_fc1[:, e:e + 2], fc1_w[e:e + 2].rearrange("e (r p) c -> p e r c", p=128)).then_inc(fc_loaded, 16)
                sp.dma_start(raw_fc2[:, e:e + 2], fc2_w[e:e + 2].rearrange("e d (r c) -> d e r c", c=C)).then_inc(fc_loaded, 16)
            spread(STEPS - 1)
            for e in range(E):
                sp.wait_ge(out_made, e + 1)
                sp.dma_start(out_d[e], out_sb[e % 2][:, :, :]).then_inc(out_stored[e % 2], 16)
            for stored in out_stored:
                sp.wait_ge(stored, 16 * E // 2)

        @block.tensor
        def _(pe):
            pe.wait_ge(consts_made, 1)
            pe.wait_ge(tables_loaded, 32)
            pe.transpose(bank(2)[:, 0:VOCAB], emb_sb[:, :], ident[0:VOCAB, 0:VOCAB])
            pe.wait_ge(diag_made, TAPS)
            for t in range(TAPS):
                last = pe.transpose(bank(2)[:, (t + 1) * C:(t + 2) * C], conv_diag[:, t, :], ident[:, :])
            last.then_inc(turned, 1)
            pe.wait_ge(tables_sb, 2)
            pe.matmul(bank(3)[0:VOCAB, 0:TAPS * C], embT[:, :], convT[:, :], start=True, stop=True).then_inc(folded_ready, 1)
            pe.wait_ge(w_loaded, 64)
            for w, k in enumerate((4, 5, 2)):
                for r in range(PAIRS):
                    last = pe.transpose(bank(k)[:, r * 128:(r + 1) * 128], raw_w[:, w, r, :], ident[:, :])
                last.then_inc(turned, 1)

            pe.wait_ge(folded_sb, 1)
            for g in range(NG):
                if g % (NG // B) == 0:
                    pe.wait_ge(onehot_made, g * B // NG + 2)
                for j in range(GROUP):
                    b, c0 = divmod((g * GROUP + j) * CHUNK, S)
                    for t in range(TAPS):
                        last = pe.matmul(bank(CONV_BANK[g])[:, j * C:(j + 1) * C], onehot[:, b, c0 + t:c0 + t + CHUNK],
                                         folded[:, t * C:(t + 1) * C], start=(t == 0), stop=(t == TAPS - 1))
                last.then_inc(conv_filled, 1)

            for r in range(PAIRS):
                last = pe.transpose(bank(3)[:, r * C:(r + 1) * C], raw_wo[:, r, :], ident[:, :])
            last.then_inc(turned, 1)
            pe.wait_ge(small_loaded, 16 * 8)
            pe.wait_ge(weights_sb, 1)
            for i in range(2):
                pe.transpose(bank(4)[:, i * C:(i + 1) * C], raw_small[:, i, :], ident[:, :])
            pe.transpose(bank(4)[:, 2 * C:2 * C + 43], raw_bias[:, :], ident[0:43, 0:43]).then_inc(turned, 1)

            def x_to_features(g):
                for j in range(GROUP):
                    last = pe.transpose(bank(CONV_BANK[g])[:, j * CHUNK:(j + 1) * CHUNK], x1[:, g * GROUP + j, :], ident[:, :])
                last.then_inc(xt_filled, 1)

            def values(t):
                if t < 2:
                    pe.wait_ge(x_rest, NG)
                    pe.wait_ge(wv_rest, 1)
                else:
                    pe.wait_ge(v_sb, t - 1)
                rows = slice(t * CHUNK, (t + 1) * CHUNK)
                for i, (xs, ws) in enumerate(((xR, wvR), (xL, wvR), (xR, wvL))):
                    last = pe.matmul(bank(6 + t % 2), xs[:, rows], ws[:, :], start=(i == 0), stop=(i == 2))
                last.then_inc(v_filled, 1)

            pe.wait_ge(x_normed, KCH)
            for g in range(NG // B):
                x_to_features(g)

            def prep_item(item, slot, p, v, token0):
                kind = item[0]
                if kind in "qk":
                    if kind == "k":
                        pe.wait_ge(w_staged, v * 2 + 2)
                    w = "qk".index(kind)
                    for half in range(2):
                        cols = bass.ds(token0 + half * BANK, BANK)
                        for i, (ws, xs) in enumerate(((w_stR, xR), (w_stL, xR), (w_stR, xL))):
                            last = pe.matmul(slot[:, half * BANK:(half + 1) * BANK], ws[:, w, :], xs[:, cols],
                                             start=(i == 0), stop=(i == 2))
                elif kind == "max":
                    _, h, qc = item
                    if h == 0 and qc == 0:
                        pe.wait_ge(k_doubled, v * 32 + 32)
                        pe.wait_ge(split, v * 4 + 4)
                    for half in range(2):
                        cols = slice(half * BANK, (half + 1) * BANK)
                        last = pe.matmul(slot[:, cols], q_full[p][h][:, qc * CHUNK:(qc + 1) * CHUNK],
                                         k_round[p][h][:, cols], start=True, stop=True)
                else:
                    pe.wait_ge(maxed, v * 2 * KCH + 2 * KCH)
                    for h in range(2):
                        last = pe.transpose(slot[0:KCH, h * BANK:h * BANK + CHUNK], maxes[h][:, :], ident[:, :])
                last.then_inc(filled, 1)

            def pe_step(s, p, prepare, s_is_first=False):
                token0 = (((s + 2) // PAIRS) % B) * S if prepare else 0
                if s_is_first:
                    earlier = PROLOGUE
                else:
                    earlier = [(i, s - 1) for i, n in numbered(True) if n is not None]
                emptied = [release(i, es) for i, es in earlier[-SLOTS:]]
                for item, n in numbered(prepare):
                    if n is None:
                        _, kc, half = item
                        if half == 0:
                            pe.wait_ge(exped, s * 2 * KCH + (2 * kc + 2))
                            if kc == 0:
                                pe.wait_ge(v_staged, s + 1)
                                if not s_is_first:
                                    pe.wait_ge(o_copied, s)
                        cols = slice(half * BANK, (half + 1) * BANK)
                        for h in range(2):
                            last = pe.matmul(acc_o[h * D:(h + 1) * D, cols], v_st[p][:, kc, h * D:(h + 1) * D],
                                             probs[h][kc % 2][:, cols], start=(kc == 0), stop=(kc == KCH - 1))
                        last.then_inc(pv_done, 1)
                        continue
                    slot = slots[slot_of(n)]
                    pe.wait_ge(*emptied[n])
                    emptied.append(release(item, s))
                    if item[0] == "exp":
                        _, kc, h = item
                        if kc == 0:
                            pe.wait_ge(q_doubled[p], (s - p) * 16 + 32)
                            pe.wait_ge(rows_loaded, s * 32 + 32)
                        keys = slice(kc * CHUNK, (kc + 1) * CHUNK)
                        for i, (ks, qs) in enumerate(((k_round, q_full), (k_rest, q_max))):
                            for half in range(2):
                                cols = slice(half * BANK, (half + 1) * BANK)
                                last = pe.matmul(slot[:, cols], ks[p][h][:, keys], qs[p][h][:, cols],
                                                 start=(i == 0), stop=(i == 1))
                        last.then_inc(filled, 1)
                    elif item[0] == "den":
                        for h in range(2):
                            pe.wait_ge(summed[h], (s + 1) * (KCH - 1))
                        for h in range(2):
                            for half in range(2):
                                quad = 32 * (2 * h + half)
                                last = pe.matmul(slot[quad:quad + 32, 0:BANK], ones32[:, :],
                                                 sums[h][:, half * BANK:(half + 1) * BANK], start=True, stop=True)
                        last.then_inc(filled, 1)
                    else:
                        prep_item(item, slot, parity(item, p), target(item, s), token0)

            emptied = []
            for n, (item, s) in enumerate(PROLOGUE):
                if n == 0:
                    pe.wait_ge(x_rest, NG // B)
                elif n == 1:
                    pe.wait_ge(weights_sb, 5)
                    pe.wait_ge(wv_rest, 1)
                elif n == 2:
                    pe.wait_ge(x_normed, 2 * KCH)
                    for g in range(NG // B, NG):
                        x_to_features(g)
                    pe.wait_ge(small_sb, 1)
                    pe.wait_ge(pads_made, 1)
                if n >= SLOTS:
                    pe.wait_ge(*emptied[n - SLOTS])
                emptied.append(release(item, s))
                prep_item(item, slots[n % SLOTS], target(item, s) % 2, target(item, s), 0)
                if item[0] == "max":
                    values(item[1] * KCH + item[2])
            pe_step(0, 0, True, s_is_first=True)
            with pe.Fori(1, STEPS - 2, 2) as it:
                pe_step(it, 1, True)
                pe_step(it + 1, 0, True)
            pe_step(STEPS - 1, 1, False)

            def fct(k):
                if k >= 4:
                    pe.wait_ge((fct_even_sb, fct_odd_sb)[k % 2], (k - 4) // 2 + 1)
                pe.wait_ge(fc_loaded, 16 * 2 * E // 2)
                raw = raw_fc1 if k % 2 == 0 else raw_fc2
                for r in range(HC):
                    last = pe.transpose(bank(k % 4)[:, r * C:(r + 1) * C], raw[:, k // 2, r, :], ident[:, :])
                last.then_inc(fct_filled, 1)

            pe.wait_ge(o_copied, STEPS)
            pe.wait_ge(den_copied, STEPS)
            for g in range(NG):
                if g < NG // B:
                    pe.wait_ge(normalised, PAIRS)
                else:
                    if g == NG // B:
                        for k in range(4):
                            fct(k)
                    pe.wait_ge(normalised, STEPS)
                for j in range(GROUP):
                    b, kc = divmod(g * GROUP + j, KCH)
                    for r in range(PAIRS):
                        last = pe.matmul(bank(4 + g)[:, j * C:(j + 1) * C],
                                         attn_out[:, b * PAIRS + r, kc * CHUNK:(kc + 1) * CHUNK], woT[:, r, :],
                                         start=(r == 0), stop=(r == PAIRS - 1))
                last.then_inc(wo_filled, 1)
            for k in range(4, 8):
                fct(k)
            for g in range(NG):
                pe.wait_ge(ln_out, GROUP * (2 * g + 2))
                for j in range(GROUP):
                    last = pe.transpose(bank(4 + g)[:, j * CHUNK:(j + 1) * CHUNK], normed2[:, g * GROUP + j, :], ident[:, :])
                last.then_inc(nt_filled, 1)
                fct(8 + 2 * g)
                fct(9 + 2 * g)
                pe.wait_ge(normT_made, g + 1)
                pe.matmul(bank(4 + g), attn_wT, normT[g % 2][:, :], start=True, stop=False, skip_group_check=True)
                for j in range(GROUP):
                    last = pe.matmul(bank(4 + g)[:, j * CHUNK:(j + 1) * CHUNK], h1n[:, g * GROUP + j, :], ident[:, :],
                                     start=False, stop=True, skip_group_check=True)
                last.then_inc(xa_filled, 1)

            def hidden(e):
                if e == 0:
                    pe.wait_ge(fct_even_sb, E)
                    pe.wait_ge(fct_odd_sb, E)
                    pe.wait_ge(xa_made, NG)
                if e >= SLOTS:
                    pe.wait_ge(hid_made, HC * (e - SLOTS + 1))
                toks = xaT[:, :].rearrange("c (b n) -> c b n", b=B)[:, :, e * CHUNK:(e + 1) * CHUNK]
                slot = slots[e % SLOTS][:, :].rearrange("p (r b n) -> p r b n", r=HC, b=B)
                for r in range(HC):
                    last = pe.matmul(slot[:, r], fc1T[:, e, r, :], toks, start=True, stop=True)
                last.then_inc(hid_filled, 1)

            def second(e):
                pe.wait_ge(hid_made, HC * (e + 1))
                if e >= 2:
                    pe.wait_ge(z_biased, e - 1)
                for r in range(HC):
                    last = pe.matmul(acc_o[:, (e % 2) * BANK:(e % 2) * BANK + B * CHUNK], fc2T[:, e, r, :],
                                     hidT[e % 2][:, r, :], start=(r == 0), stop=(r == HC - 1))
                last.then_inc(y_filled, 1)

            def third(e):
                pe.wait_ge(y_made, e + 1)
                for b in range(B):
                    o = (e % 2) * BANK + B * CHUNK + b * C
                    last = pe.matmul(acc_o[:, o:o + C], yT[e % 2][:, b * CHUNK:(b + 1) * CHUNK], next_wT,
                                     start=True, stop=True)
                last.then_inc(z_filled, 1)

            for e in range(E + 2):
                if e < E:
                    hidden(e)
                if 1 <= e <= E:
                    second(e - 1)
                if e >= 2:
                    third(e - 2)

        @block.scalar
        def _(act):
            act.dma_start(emb_sb[:, :], emb).then_inc(tables_loaded, 16)
            act.dma_start(conv_sb[:, :, :], conv_w).then_inc(tables_loaded, 16)
            act.dma_start(raw_w[:, 0], wq.rearrange("(r p) c -> p r c", p=128)).then_inc(w_loaded, 16)
            act.dma_start(raw_w[:, 1], wk.rearrange("(r p) c -> p r c", p=128)).then_inc(w_loaded, 16)
            act.wait_ge(consts_made, 1)
            for w, k in enumerate((4, 5)):
                act.wait_ge(turned, 2 + w)
                act.copy(wqk[:, :, w, :], bank(k).rearrange("c (r n) -> c r n", n=128)).then_inc(weights_sb, 1)
            act.wait_ge(turned, 4)
            act.copy(wvR[:, :], bank(2)).then_inc(weights_sb, 1)

            def relu(g):
                act.wait_ge(conv_filled, g + 1)
                act.activation(h0[:, g * GROUP:(g + 1) * GROUP, :],
                               bank(CONV_BANK[g]).rearrange("p (t c) -> p t c", c=C), ACT.Relu).then_inc(h0_made, 1)

            def x_round(g):
                act.wait_ge(xt_filled, g + 1)
                act.copy(xR[:, g * BANK:(g + 1) * BANK], bank(CONV_BANK[g])).then_inc(x_rounded, 1)

            def x_sqrt(b):
                act.wait_ge(x_aggr, KCH * (b + 1))
                act.activation(std[:, :], mv[:, :, 1], ACT.Sqrt, bias=eps[:, 0:1]).then_inc(x_std, 1)

            relu(0)
            relu(1)
            x_sqrt(0)
            relu(2)
            relu(3)
            act.wait_ge(turned, 5)
            act.copy(woT[:, :, :], bank(3).rearrange("p (r c) -> p r c", c=C)).then_inc(weights_sb, 2)
            x_round(0)
            x_round(1)
            x_sqrt(1)

            def act_item(item, count, slot, p, s, first):
                kind = item[0]
                if kind == "exp":
                    _, kc, h = item
                    act.wait_ge(filled, count)
                    if not (first and kc < 2):
                        act.wait_ge(pv_done, s * 2 * KCH + 2 * (kc - 1))
                        act.wait_ge(summed[h], s * (KCH - 1) + adds_before_reuse(kc))
                    act.activation(probs[h][kc % 2][:, :], slot[:, :], ACT.Exp, scale=SCALE).then_inc(exped, 1)
                elif kind in "qk":
                    act.wait_ge(filled, count)
                    for h in range(2):
                        act.copy((q_full if kind == "q" else k_round)[p][h][0:D, :],
                                 slot[h * D:(h + 1) * D, :]).then_inc(rounded, 1)
                elif kind == "den":
                    act.wait_ge(pv_done, s * 2 * KCH + 2 * KCH)
                    if not first:
                        act.wait_ge(normalised, s)
                    act.copy(o_sb[:, :], acc_o[:, :]).then_inc(o_copied, 1)
                    act.wait_ge(filled, count)
                    act.copy(den_sb[:, :], slot[:, 0:BANK]).then_inc(den_copied, 1)

            def act_step(s, p, prepare, first=False):
                for item, n in numbered(prepare):
                    if n is not None:
                        act_item(item, item_count(s, n), slots[slot_of(n)], parity(item, p), s, first)

            act.wait_ge(pads_made, 1)
            for n, (item, s) in enumerate(PROLOGUE):
                act_item(item, n + 1, slots[n % SLOTS], target(item, s) % 2, s, True)
                if n == 1:
                    x_round(2)
                    x_round(3)
                if item[0] == "max":
                    t = item[1] * KCH + item[2]
                    b, kc = divmod(t, KCH)
                    act.wait_ge(v_filled, t + 1)
                    act.copy(v_all[:, b * PAIRS:(b + 1) * PAIRS, kc, :],
                             bank(6 + t % 2).rearrange("p (r d) -> p r d", r=PAIRS)).then_inc(v_sb, 1)
            act_step(0, 0, True, first=True)
            with act.Fori(1, STEPS - 2, 2) as it:
                act_step(it, 1, True)
                act_step(it + 1, 0, True)
            act_step(STEPS - 1, 1, False)

            def ln_sqrt(n):
                act.wait_ge(ln_aggr, GROUP * (n + 1))
                act.activation(std[:, 0:GROUP], mv[:, 0:GROUP, 1], ACT.Sqrt, bias=eps[:, 0:1]).then_inc(ln_std, 1)

            def fct_copy(k):
                act.wait_ge(fct_filled, k + 1)
                if k == 0:
                    act.wait_ge(normalised, STEPS)
                act.copy(fc1T[:, k // 2, :, :], bank(k % 4).rearrange("p (r c) -> p r c", c=C)).then_inc(fct_even_sb, 1)

            def norm_t(g):
                act.wait_ge(nt_filled, g + 1)
                if g >= 2:
                    act.wait_ge(xa_filled, g - 1)
                act.activation(normT[g % 2][:, :], bank(4 + g), ACT.Identity, bias=b_col, scale=g_col).then_inc(normT_made, 1)

            def xa_copy(g):
                act.wait_ge(xa_filled, g + 1)
                act.activation(xaT[:, g * BANK:(g + 1) * BANK], bank(4 + g), ACT.Identity, bias=attn_b_col).then_inc(xa_made, 1)

            act.wait_ge(o_copied, STEPS)
            for what, i in (("ln", 0), ("fct", 0), ("fct", 2), ("ln", 1), ("fct", 4), ("fct", 6), ("nt", 0),
                            ("ln", 2), ("fct", 8), ("xa", 0), ("nt", 1), ("fct", 10),
                            ("ln", 3), ("xa", 1), ("nt", 2), ("fct", 12), ("xa", 2), ("nt", 3), ("fct", 14), ("xa", 3)):
                if what == "ln":
                    ln_sqrt(2 * i)
                    ln_sqrt(2 * i + 1)
                elif what == "fct":
                    fct_copy(i)
                elif what == "nt":
                    norm_t(i)
                else:
                    xa_copy(i)

            for e in range(E + 2):
                if e < E:
                    act.wait_ge(hid_filled, e + 1)
                    if e >= 2:
                        act.wait_ge(y_filled, e - 1)
                    slot = slots[e % SLOTS][:, :].rearrange("p (r n) -> p r n", r=HC)
                    for r in range(HC):
                        act.activation(hidT[e % 2][:, r, :], slot[:, r, :], ACT.Gelu,
                                       bias=fc1_b_col[:, e * HC + r:e * HC + r + 1]).then_inc(hid_made, 1)
                if e >= 2:
                    act.wait_ge(z_biased, e - 1)
                    if e >= 4:
                        act.wait_ge(out_made, e - 3)
                    act.activation(z_act[e % 2][:, :, :], z_pre[e % 2][:, :, :], ACT.Gelu).then_inc(z_made, 1)

        @block.vector
        def _(dve):
            dve.wait_ge(consts_made, 1)
            dve.tensor_copy(iota_f[:, :], iota_i[:, :]).then_inc(iota_cast, 1)
            dve.memset(onehot[:, :, 0:1], 0.0).then_inc(onehot_made, 1)
            dve.wait_ge(tables_loaded, 32)
            for t in range(TAPS):
                dve.tensor_tensor(conv_diag[:, t, :].rearrange("o (g i) -> o g i", i=4),
                                  conv_sb[:, :, t].unsqueeze(1).broadcast_to([C, 32, 4]),
                                  group_mask[:, :].unsqueeze(2).broadcast_to([C, 32, 4]), ALU.mult).then_inc(diag_made, 1)
            dve.wait_ge(iota_cast, 1)
            dve.wait_ge(ids_loaded, 16 * B)
            for b in range(B):
                dve.tensor_scalar(onehot[:, b, 1:S + 1], ids[:, b * S:(b + 1) * S], float(VOCAB - 1),
                                  iota_f[0:VOCAB, 0:1], ALU.min, ALU.is_equal).then_inc(onehot_made, 1)
            dve.wait_ge(turned, 1)
            dve.tensor_copy(embT[:, :], bank(2)[:, 0:VOCAB]).then_inc(tables_sb, 1)
            dve.tensor_copy(convT[:, :], bank(2)[:, C:(TAPS + 1) * C]).then_inc(tables_sb, 1)
            dve.wait_ge(folded_ready, 1)
            dve.tensor_copy(folded[:, :], bank(3)[0:VOCAB, 0:TAPS * C]).then_inc(folded_sb, 1)
            dve.wait_ge(weights_sb, 3)
            dve.tensor_tensor(wvL[:, :], bank(2), wvR[:, :].bitcast(F32), ALU.subtract).then_inc(wv_rest, 1)

            def norm_x(b):
                own = range(b * KCH, (b + 1) * KCH)
                for j, t in enumerate(own):
                    if j % GROUP == 0:
                        dve.wait_ge(h0_made, t // GROUP + 1)
                    dve.bn_stats(stats[:, j, :], h0[:, t, :]).then_inc(x_stats, 1)
                if b:
                    dve.wait_ge(x_normed, KCH * b)
                for j in range(KCH):
                    dve.wait_ge(x_stats, KCH * b + j + 1)
                    dve.bn_aggr(mv[:, j, :], stats[:, j, :]).then_inc(x_aggr, 1)
                dve.wait_ge(x_std, b + 1)
                dve.reciprocal(rstd[:, :], std[:, :]).then_inc(x_rstd, 1)
                dve.wait_ge(x_rstd, b + 1)
                for j, t in enumerate(own):
                    dve.tensor_scalar(x1[:, t, :], h0[:, t, :], mv[:, j, 0:1], rstd[:, j:j + 1],
                                      ALU.subtract, ALU.mult).then_inc(x_normed, 1)

            def x_rests(g):
                dve.wait_ge(x_rounded, g + 1)
                dve.tensor_tensor(xL[:, g * BANK:(g + 1) * BANK], bank(CONV_BANK[g]),
                                  xR[:, g * BANK:(g + 1) * BANK].bitcast(F32), ALU.subtract).then_inc(x_rest, 1)

            def stage_w(v):
                src = wqk[:, v % PAIRS, :, :]
                dve.tensor_copy(w_stR[:, :, :], src).then_inc(w_staged, 1)
                dve.wait_ge(w_staged, v * 2 + 1)
                dve.tensor_tensor(w_stL[:, :, :], src, w_stR[:, :, :].bitcast(F32), ALU.subtract).then_inc(w_staged, 1)

            def dve_item(item, count, slot, p, s, first=False):
                kind = item[0]
                if kind == "exp":
                    _, kc, h = item
                    if h == 1 and kc >= POOL_ADDS:
                        dve.wait_ge(exped, s * 2 * KCH + (2 * kc + 1))
                        dve.wait_ge(summed[0], s * (KCH - 1) + (kc - 1))
                        dve.tensor_tensor(sums[0][:, :], sums[0][:, :], probs[0][kc % 2][:, :], ALU.add).then_inc(summed[0], 1)
                elif kind in "qk":
                    whole = q_full if kind == "q" else k_round
                    for h in range(2):
                        rest = q_full[p][h][D:128, :] if kind == "q" else k_rest[p][h][0:D, :]
                        dve.wait_ge(rounded, target(item, s) * 4 + (h + (1 if kind == "k" else 3)))
                        dve.tensor_tensor(rest, slot[h * D:(h + 1) * D, :], whole[p][h][0:D, :].bitcast(F32),
                                          ALU.subtract).then_inc(split, 1)
                elif kind == "max":
                    _, h, qc = item
                    dve.wait_ge(filled, count)
                    dve.reduce_max(maxes[h][:, qc:qc + 1], slot[:, :], AX.X).then_inc(maxed, 1)
                elif kind == "rows":
                    dve.wait_ge(filled, count)
                    if not first:
                        dve.wait_ge(rows_loaded, target(item, s) * 32)
                    dve.tensor_scalar(neg_max[:, :, :], slot[0:KCH, :].rearrange("c (h n) -> c h n", h=2)[:, :, 0:CHUNK],
                                      -1.0, None, ALU.mult).then_inc(rows_made, 1)

            def invert(s):
                dve.wait_ge(den_spread, s * 16 + 16)
                dve.reciprocal(inv_flat[:, :], den_flat[:, :]).then_inc(inverted, 1)

            def stage_v(v, p):
                dve.tensor_copy(v_st[p][:, :, :], v_all[:, v, :, :]).then_inc(v_staged, 1)

            def dve_step(s, p, prepare, first=False):
                items = list(numbered(prepare))
                if prepare:
                    k, rows = (next(i for i, (item, _) in enumerate(items) if item == (kind,)) for kind in ("k", "rows"))
                    items[k], items[rows] = items[rows], items[k]
                for item, n in items:
                    if item == ("pv", 0, 1):
                        if not first:
                            invert(s - 1)
                        if prepare:
                            if not first:
                                dve.wait_ge(pv_done, s * 2 * KCH)
                            stage_v(s + 1, 1 - p)
                    if n is not None:
                        dve_item(item, item_count(s, n), slots[slot_of(n)], parity(item, p), s)
                    if item == ("max", 0, 2):
                        stage_w(s + 2)

            norm_x(0)
            dve.wait_ge(weights_sb, 2)
            stage_w(0)
            dve.wait_ge(turned, 6)
            dve.tensor_copy(small[:, :], bank(4)[:, 0:2 * C + 43]).then_inc(small_sb, 1)
            x_rests(0)
            x_rests(1)
            norm_x(1)
            dve.wait_ge(pads_made, 1)
            for n, (item, s) in enumerate(PROLOGUE):
                dve_item(item, n + 1, slots[n % SLOTS], target(item, s) % 2, s, True)
                if n == 1:
                    x_rests(2)
                    x_rests(3)
                if item == ("max", 0, 2):
                    stage_w(1)
            dve.wait_ge(v_sb, NCH)
            stage_v(0, 0)
            dve_step(0, 0, True, first=True)
            with dve.Fori(1, STEPS - 2, 2) as it:
                dve_step(it, 1, True)
                dve_step(it + 1, 0, True)
            dve_step(STEPS - 1, 1, False)
            invert(STEPS - 1)

            def layernorm(n, src, dst):
                if n:
                    dve.wait_ge(ln_out, GROUP * n)
                for j in range(GROUP):
                    dve.bn_stats(stats[:, j, :], src[:, j, :]).then_inc(ln_stats, 1)
                for j in range(GROUP):
                    dve.wait_ge(ln_stats, GROUP * n + j + 1)
                    dve.bn_aggr(mv[:, j, :], stats[:, j, :]).then_inc(ln_aggr, 1)
                dve.wait_ge(ln_std, n + 1)
                dve.reciprocal(rstd[:, 0:GROUP], std[:, 0:GROUP]).then_inc(ln_rstd, 1)
                dve.wait_ge(ln_rstd, n + 1)
                for j in range(GROUP):
                    dve.tensor_scalar(dst[:, j, :], src[:, j, :], mv[:, j, 0:1], rstd[:, j:j + 1],
                                      ALU.subtract, ALU.mult).then_inc(ln_out, 1)

            def fct_copy(k):
                dve.wait_ge(fct_filled, k + 1)
                if k == 1:
                    dve.wait_ge(normalised, STEPS)
                dve.tensor_copy(fc2T[:, k // 2, :, :], bank(k % 4).rearrange("p (r c) -> p r c", c=C)).then_inc(fct_odd_sb, 1)

            for g in range(NG):
                own = slice(g * GROUP, (g + 1) * GROUP)
                dve.wait_ge(wo_filled, g + 1)
                dve.wait_ge(residual_made, NG)
                dve.tensor_tensor(residual[:, own, :], bank(4 + g).rearrange("p (t c) -> p t c", c=C),
                                  residual[:, own, :], ALU.add).then_inc(h1_made, 1)
                dve.wait_ge(h1_made, g + 1)
                layernorm(2 * g, residual[:, own, :], h1n[:, own, :])
                layernorm(2 * g + 1, h1n[:, own, :], normed2[:, own, :])
                for k in (4 * g + 1, 4 * g + 3):
                    fct_copy(k)

            for e in range(E + 1):
                if e < E:
                    dve.wait_ge(y_filled, e + 1)
                    dve.tensor_scalar(yT[e % 2][:, :], acc_o[:, (e % 2) * BANK:(e % 2) * BANK + B * CHUNK],
                                      fc2_b_col[:, e:e + 1], None, ALU.add).then_inc(y_made, 1)
                if e >= 1:
                    i = (e - 1) % 2
                    dve.wait_ge(z_filled, e)
                    if e >= 3:
                        dve.wait_ge(z_made, e - 2)
                    dve.tensor_tensor(z_pre[i][:, :, :],
                                      acc_o[:, i * BANK + B * CHUNK:(i + 1) * BANK].rearrange("p (b c) -> p b c", b=B),
                                      next_b_row[:, :].unsqueeze(1).broadcast_to([128, B, C]), ALU.add).then_inc(z_biased, 1)

        @block.gpsimd
        def _(pool):
            pool.memset(ident[:, :], 0.0).then_inc(zeroed, 1)
            pool.memset(group_mask[:, :], 1.0).then_inc(zeroed, 1)
            pool.memset(ones32[:, :], 1.0)
            pool.memset(eps[:, :], EPS)
            pool.iota(iota_i[:, :], pattern=[[0, 1]], base=0, channel_multiplier=1)
            pool.wait_ge(zeroed, 2)
            pool.affine_select(out=group_mask[:, :], in_=group_mask[:, :], compare_op=ALU.is_ge, fill=0.0, base=0,
                               pattern=[[-4, 32]], channel_multiplier=1).then_inc(zeroed, 1)
            pool.wait_ge(zeroed, 3)
            pool.affine_select(out=group_mask[:, :], in_=group_mask[:, :], compare_op=ALU.is_ge, fill=0.0, base=3,
                               pattern=[[4, 32]], channel_multiplier=-1)
            pool.affine_select(out=ident[:, :], in_=ident[:, :], compare_op=ALU.not_equal, fill=1.0, base=0,
                               pattern=[[-1, 128]], channel_multiplier=1).then_inc(consts_made, 1)
            for p in range(2):
                for h in range(2):
                    pool.memset(q_max[p][h][:, :].bitcast(F32), 0.0)
                    last = pool.memset(k_rest[p][h][:, :].bitcast(F32), 1.0)
            last.then_inc(pads_made, 1)

            for g in range(NG):
                own = slice(g * GROUP, (g + 1) * GROUP)
                pool.wait_ge(x_normed, GROUP * (g + 1))
                pool.wait_ge(onehot_made, B + 1)
                pool.tensor_tensor(residual[:, own, :], h0[:, own, :], x1[:, own, :], ALU.add).then_inc(residual_made, 1)

            def normalise(s):
                pool.wait_ge(inv_loaded, s * 32 + 32)
                pool.tensor_tensor(attn_out[:, s, :], o_sb[:, :], inv_sb[:, :], ALU.mult).then_inc(normalised, 1)

            def pool_step(s, p, prepare, first=False):
                for kc in range(1, KCH):
                    if kc == 6 and not first:
                        normalise(s - 1)
                    for h in range(2):
                        if h == 0 and kc >= POOL_ADDS:
                            continue
                        pool.wait_ge(exped, s * 2 * KCH + (2 * kc + h + 1))
                        if kc == 1 and not first:
                            pool.wait_ge(den_copied, s)
                        if kc > 1:
                            pool.wait_ge(summed[h], s * (KCH - 1) + (kc - 1))
                        before = probs[h][0] if kc == 1 else sums[h]
                        pool.tensor_tensor(sums[h][:, :], before[:, :], probs[h][kc % 2][:, :], ALU.add).then_inc(summed[h], 1)

            pool_step(0, 0, True, first=True)
            with pool.Fori(1, STEPS - 2, 2) as it:
                pool_step(it, 1, True)
                pool_step(it + 1, 0, True)
            pool_step(STEPS - 1, 1, False)

            normalise(STEPS - 1)

            h1 = residual[:, :, :].rearrange("p (b e) c -> p b e c", b=B)
            for e in range(E):
                pool.wait_ge(z_made, e + 1)
                if e >= 2:
                    pool.wait_ge(out_stored[e % 2], 16 * (e // 2))
                pool.tensor_tensor(out_sb[e % 2][:, :, :], z_act[e % 2][:, :, :], h1[:, :, e, :], ALU.add).then_inc(out_made, 1)


_INS = ["x", "L0_tok_emb_table", "L0_tok_conv_w", "L0_attn_Wq", "L0_attn_Wk", "L0_attn_Wv", "L0_attn_Wo",
        "L0_ffn_ln_g", "L0_ffn_ln_b", "L0_ffn_attn_w", "L0_ffn_attn_b", "L0_ffn_fc1_w", "L0_ffn_fc1_b",
        "L0_ffn_fc2_w", "L0_ffn_fc2_b", "L0_ffn_next_w", "L0_ffn_next_b"]
_OUT = ((2, 1024, 128), "float32")


def kernel(**inputs):
    import numpy as np
    import concourse.bacc as bacc
    from concourse.bass_utils import run_bass_kernel_spmd

    nc = bacc.Bacc("TRN2", target_bir_lowering=False, num_devices=1)
    arrays, args = {}, []
    for name in _INS:
        a = np.ascontiguousarray(inputs[name])
        arrays[f"in_{name}"] = a
        args.append(nc.dram_tensor(f"in_{name}", a.shape, mybir.dt.from_np(a.dtype), kind="ExternalInput").ap())
    args.append(nc.dram_tensor("out_h", _OUT[0], mybir.dt.from_np(np.dtype(_OUT[1])), kind="ExternalOutput").ap())
    build(nc, *args)
    r = run_bass_kernel_spmd(nc, [arrays], core_ids=[0])
    return r.results[0]["out_h"]
```

```python
from contextlib import ExitStack

import concourse.bass as bass
from concourse import mybir

F32 = mybir.dt.float32
F32R = mybir.dt.float32r
I32 = mybir.dt.int32
ALU = mybir.AluOpType
ACT = mybir.ActivationFunctionType
AX = mybir.AxisListType

C = 128
B, S = 2, 1024
HEADS, D = 8, 64
PAIRS = HEADS // 2
STEPS = B * PAIRS
CHUNK = 128
NCH = B * S // CHUNK
KCH = S // CHUNK
GROUP = 4
NG = NCH // GROUP
E, HID = 8, 512
HC = HID // 128
DUOS = B * E // 2
TAPS = 2
EPS = 1e-5
SCALE = float(D) ** -0.5
BANK = 512
SLOTS = 3
CONV_BANK = (0, 1, 6, 7)
POOL_ADDS = 3


MAXES = [("max", h, qc) for h in range(2) for qc in range(KCH)]
MAXES_IN = (0, 2, 3, 3, 3, 2, 2, 1)
assert sum(MAXES_IN) == len(MAXES)

PROLOGUE = ([(("k",), -2), (("q",), -2)] + [(item, -1) for item in MAXES]
            + [(("rows",), -1), (("k",), -1), (("q",), -1)])
WARM_START, WARM_SPLIT = 12, 12
V_FROM = 5
EARLY = 6
LAST_EXTRA = [[("wo",)], [("fct", 0)], [("fct", 1)], [("fct", 2)], [("nt",)], [("fct", 3), ("fct", 4)], [("xa",)], [("fct", 5)]]


def step_order(prepare):
    order = []
    for kc in range(KCH):
        at = sum(MAXES_IN[:kc])
        extra = MAXES[at:at + MAXES_IN[kc]]
        pv = [("pv", kc - 1, half) for half in range(2 if kc else 0)]
        if not prepare:
            order += [("exp", kc, 0), ("exp", kc, 1)] + pv[:1] + LAST_EXTRA[kc] + pv[1:]
            continue
        order += [("exp", kc, 0)] + extra[:1] + [("exp", kc, 1)] + pv[:1] + extra[1:] + pv[1:]
    if prepare:
        return order + [("k",), ("rows",), ("q",), ("pv", KCH - 1, 0), ("pv", KCH - 1, 1), ("den",)]
    return order + [("pv", KCH - 1, 0), ("pv", KCH - 1, 1), ("last den",)] + [("fct", e) for e in range(EARLY, E)]


def values_after(n):
    if n == len(PROLOGUE) - 1:
        return range(n - V_FROM, NCH)
    return [n - V_FROM] if n >= V_FROM else []


ITEMS = len([i for i in step_order(True) if i[0] != "pv"])
assert ITEMS % SLOTS == 0


def numbered(prepare=True):
    n = 0
    for item in step_order(prepare):
        if item[0] == "pv":
            yield item, None
        else:
            yield item, n
            n += 1


def item_count(s, n):
    return s * ITEMS + (len(PROLOGUE) + n + 1)


def slot_of(n):
    return (len(PROLOGUE) + n) % SLOTS


SUMS_SLOT, ODD_SLOT, LAST_SLOT = (slot_of(n) for _, n in list(numbered(False))[-3:])


def target(item, s):
    return s + {"q": 2, "k": 2, "max": 1, "rows": 1}.get(item[0], 0)


def parity(item, p):
    return 1 - p if item[0] in ("max", "rows") else p


def adds_before_reuse(kc):
    return kc - 1 if kc < 2 else max(kc - 2, 1)


def build(nc, x, emb, conv_w, wq, wk, wv, wo, ln_g, ln_b, attn_w, attn_b,
          fc1_w, fc1_b, fc2_w, fc2_b, next_w, next_b, out):
    VOCAB = emb.shape[0]
    with ExitStack() as ctx:
        def sem(name):
            return ctx.enter_context(nc.semaphore(name))

        def sb(name, shape, dt=F32, scope=ctx):
            return scope.enter_context(nc.sbuf_tensor(name, shape, dt))

        slots = [ctx.enter_context(nc.psum_tensor(f"slot{i}", [128, 2 * BANK], F32)) for i in range(SLOTS)]
        acc_o = ctx.enter_context(nc.psum_tensor("acc_o", [128, 2 * BANK], F32))

        def bank(k):
            t = slots[k // 2] if k < 2 * SLOTS else acc_o
            return t[:, (k % 2) * BANK:(k % 2 + 1) * BANK]

        ident = sb("ident", [128, 128])
        ones = sb("ones", [128, D])
        iota_i = sb("iota_i", [128, 1], I32)
        iota_f = sb("iota_f", [128, 1])
        eps = sb("eps", [128, 1])
        eps_squared = sb("eps_squared", [128, 1])
        table_warmer = sb("table_warmer", [128, 2])
        group_mask = sb("group_mask", [128, 32])
        woT = sb("woT", [128, PAIRS, C])
        small = sb("small", [128, 2 * C + 43])
        next_b_row = sb("next_b_row", [128, C])
        stats = sb("stats", [128, KCH, 6])
        mv = sb("mv", [128, KCH, 2])
        std = sb("std", [128, 2, KCH])
        rstd = sb("rstd", [128, 2, KCH])
        residual = sb("residual", [128, NCH, C])
        attn_out = sb("attn_out", [128, STEPS, S])
        v_all = sb("v_all", [128, STEPS, KCH, 2 * D])

        with ExitStack() as front:
            emb_sb = sb("emb_sb", [VOCAB, C], F32, front)
            conv_sb = sb("conv_sb", [C, 4, TAPS], F32, front)
            conv_diag = sb("conv_diag", [C, TAPS, C], F32, front)
            embT = sb("embT", [C, 128], F32, front)
            convT = sb("convT", [C, TAPS * C], F32, front)
            folded = sb("folded", [128, TAPS * C], F32, front)
            wvR = sb("wvR", [C, HEADS * D], F32R, front)
            wvL = sb("wvL", [C, HEADS * D], F32R, front)
            raw_small = sb("raw_small", [128, 2, C], F32, front)
            raw_bias = sb("raw_bias", [43, C], F32, front)
        with ExitStack() as att:
            sums = [sb(f"sums{h}", [128, S], F32, att) for h in range(2)]
            den_sb = sb("den_sb", [128, BANK], F32, att)
            den_flat = sb("den_flat", [128, 2 * S // 128], F32, att)
            inv_flat = sb("inv_flat", [128, 2 * S // 128], F32, att)
            inv_sb = sb("inv_sb", [128, S], F32, att)
            o_sb = sb("o_sb", [128, S], F32, att)

            def operands(p, scope):
                return [[sb(f"{name}{p}{h}", [128, S], F32R, scope) for h in range(2)]
                        for name in ("q_full", "q_max", "k_round", "k_rest")]

            probs = [[sb(f"probs{h}{i}", [128, S], F32, att) for i in range(2)] for h in range(2)]
            maxes = [sb(f"maxes{h}", [128, KCH], F32, att) for h in range(2)]
            neg_max = sb("neg_max", [KCH, 2, CHUNK], F32R, att)
            v_st = [sb(f"v_st{p}", [128, KCH, 2 * D], F32, att) for p in range(2)]
            odd_operands = operands(1, att)
            with ExitStack() as early:
                q_full, q_max, k_round, k_rest = zip(operands(0, early), odd_operands)
                xR = sb("xR", [C, B * S], F32R, early)
                xL = sb("xL", [C, B * S], F32R, early)
                wqk = sb("wqk", [C, PAIRS, 2, 2 * D], F32, early)
                w_stR = sb("w_stR", [C, 2, 2 * D], F32R, early)
                w_stL = sb("w_stL", [C, 2, 2 * D], F32R, early)
            fcT = sb("fcT", [128, E, 2, HC, C], F32, att)
            xaT = sb("xaT", [C, B * S], F32, att)
            h1n = sb("h1n", [128, KCH, C], F32, att)
            normed2 = sb("normed2", [128, KCH, C], F32, att)
            normT = sb("normT", [C, S], F32, att)
        hidT = [probs[0][i][:, :].rearrange("p (e r n) -> p e r n", e=2, r=HC) for i in range(2)]
        yT = [probs[1][0][:, i * 2 * CHUNK:(i + 1) * 2 * CHUNK] for i in range(2)]
        z_pre = [probs[1][0][:, (i + 2) * 2 * CHUNK:(i + 3) * 2 * CHUNK].rearrange("p (e c) -> p e c", e=2) for i in range(2)]
        z_act = [probs[1][1][:, i * 2 * CHUNK:(i + 1) * 2 * CHUNK].rearrange("p (e c) -> p e c", e=2) for i in range(2)]
        out_sb = [probs[1][1][:, (i + 2) * 2 * CHUNK:(i + 3) * 2 * CHUNK].rearrange("p (e c) -> p e c", e=2) for i in range(2)]

        flat = attn_out[:, :, :].rearrange("p s n -> p (s n)")
        h0 = flat[:, 0:NCH * C].rearrange("p (t c) -> p t c", c=C)
        x1 = flat[:, NCH * C:2 * NCH * C].rearrange("p (t c) -> p t c", c=C)
        PAD = 2 * NCH * C
        onehot = flat[:, PAD:PAD + B * (S + 1)].rearrange("p (b n) -> p b n", b=B)
        ids = residual[:, :, :].bitcast(I32).rearrange("p t c -> p (t c)")
        vflat = v_all[:, :, :, :].rearrange("p s k d -> p (s k d)")
        raw_w = vflat[:, 0:3 * PAIRS * C].rearrange("p (w r c) -> p w r c", w=3, c=C)
        raw_wo = vflat[:, 3 * PAIRS * C:4 * PAIRS * C].rearrange("p (r c) -> p r c", c=C)
        FCN = E * HC * C
        raw_fc1 = vflat[:, 0:FCN].rearrange("p (e r c) -> p e r c", e=E, c=C)
        raw_fc2 = vflat[:, FCN:2 * FCN].rearrange("p (e r c) -> p e r c", e=E, c=C)
        fc1_b_col = small[:, 2 * C:2 * C + E * HC]
        fc2_b_col = small[:, 2 * C + 32:2 * C + 40]
        g_col, b_col, attn_b_col = (small[:, 2 * C + 40 + i:2 * C + 41 + i] for i in range(3))
        attn_wT, next_wT = small[:, 0:C], small[:, C:2 * C]

        ids_loaded, tables_loaded, w_loaded = sem("ids_loaded"), sem("tables_loaded"), sem("w_loaded")
        small_loaded, fc_loaded = sem("small_loaded"), sem("fc_loaded")
        out_stored = [sem("out_stored_even"), sem("out_stored_odd")]
        zeroed, consts_made = sem("zeroed"), sem("consts_made")
        iota_cast, onehot_made, diag_made = sem("iota_cast"), sem("onehot_made"), sem("diag_made")
        turned, tables_sb, folded_ready, folded_sb = sem("turned"), sem("tables_sb"), sem("folded_ready"), sem("folded_sb")
        weights_sb, wv_rest, small_sb = sem("weights_sb"), sem("wv_rest"), sem("small_sb")
        conv_filled, h0_made, residual_made = sem("conv_filled"), sem("h0_made"), sem("residual_made")
        xt_filled, x_rounded, x_rest = sem("xt_filled"), sem("x_rounded"), sem("x_rest")
        v_filled, v_sb = sem("v_filled"), sem("v_sb")
        x_stats, x_aggr, x_std, x_rstd, x_normed = (sem(n) for n in ("x_stats", "x_aggr", "x_std", "x_rstd", "x_normed"))
        x_centred, x_late_normed = sem("x_centred"), sem("x_late_normed")
        pads_made = sem("pads_made")
        filled = sem("filled")
        pv_done = sem("pv_done")
        exped = sem("exped")
        rounded = sem("rounded")
        k_doubled = sem("k_doubled")
        q_doubled = [sem("q_doubled_even"), sem("q_doubled_odd")]
        split = sem("split")
        maxed = sem("maxed")
        rows_made = sem("rows_made")
        rows_loaded = sem("rows_loaded")
        summed = [sem("summed_a"), sem("summed_b")]
        den_copied = sem("den_copied")
        o_copied = sem("o_copied")
        den_spread = sem("den_spread")
        inverted = sem("inverted")
        inv_stored = sem("inv_stored")
        inv_loaded = sem("inv_loaded")
        normalised = sem("normalised")
        w_staged = sem("w_staged")
        v_staged = sem("v_staged")
        h1_made = sem("h1_made")
        ln_stats, ln_aggr, ln_std, ln_rstd = (sem(n) for n in ("ln_stats", "ln_aggr", "ln_std", "ln_rstd"))
        n2_made = sem("n2_made")
        n1_made = sem("n1_made")
        normT_made = sem("normT_made")
        xa_made = sem("xa_made")
        fct_sb = [sem("fct_sb_dve"), sem("fct_sb_act")]
        wo_filled, nt_filled, xa_filled = sem("wo_filled"), sem("nt_filled"), sem("xa_filled")
        hid_filled, hid_made, y_filled, y_made = sem("hid_filled"), sem("hid_made"), sem("y_filled"), sem("y_made")
        z_filled, z_biased, z_made, out_made = sem("z_filled"), sem("z_biased"), sem("z_made"), sem("out_made")

        def release(item, s):
            kind, v = item[0], target(item, s)
            if kind == "exp":
                return exped, s * 2 * KCH + (2 * item[1] + item[2] + 1)
            if kind in "qk":
                return split, v * 4 + (2 if kind == "k" else 4)
            if kind == "max":
                return maxed, v * 2 * KCH + (KCH * item[1] + item[2] + 1)
            if kind == "rows":
                return rows_made, v + 1
            if kind == "wo":
                return h1_made, 2
            if kind == "nt":
                return normT_made, 1
            if kind == "xa":
                return xa_made, 2
            if kind == "fct":
                return (fct_sb[0], item[1] + 1) if item[1] < EARLY else (fct_sb[1], item[1] + 1 - EARLY)
            return (inverted, STEPS + 1) if kind == "last den" else (den_copied, s + 1)

        duo_slots, late_slot = (slots[ODD_SLOT], slots[SUMS_SLOT]), slots[LAST_SLOT]
        inv_dram = nc.dram_tensor("inv_scratch", [128, 2 * S // 128], F32, kind="Internal").ap()
        out_d = out.rearrange("b (j e p) c -> b j p e c", e=2, p=CHUNK)
        block = ctx.enter_context(nc.Block())

        @block.sync
        def _(sp):
            for b in range(B):
                sp.dma_start(ids[:, b * S:(b + 1) * S], x[b:b + 1, :].partition_broadcast(128)
                             .rearrange("p a n -> p (a n)")).then_inc(ids_loaded, 16)
            sp.dma_start(raw_w[:, 2], wv.rearrange("(r p) c -> p r c", p=128)).then_inc(w_loaded, 16)
            sp.dma_start(raw_wo, wo.rearrange("c (r e) -> c r e", e=128)).then_inc(w_loaded, 16)
            sp.dma_start(raw_small[:, 0, :], attn_w).then_inc(small_loaded, 16)
            sp.dma_start(raw_small[:, 1, :], next_w).then_inc(small_loaded, 16)
            sp.dma_start(raw_bias[0:32, :], fc1_b.rearrange("e (r p) -> (e r) p", p=128)).then_inc(small_loaded, 16)
            sp.dma_start(raw_bias[32:40, :], fc2_b).then_inc(small_loaded, 16)
            for i, vec in enumerate((ln_g, ln_b, attn_b)):
                sp.dma_start(raw_bias[40 + i:41 + i, :], vec.rearrange("(a c) -> a c", a=1)).then_inc(small_loaded, 16)
            sp.dma_start(next_b_row[:, :], next_b.rearrange("(a c) -> a c", a=1).partition_broadcast(128)
                         .rearrange("p a c -> p (a c)")).then_inc(small_loaded, 16)

            def spread(s):
                sp.wait_ge(den_copied, s + 1)
                sp.dma_start(den_flat[:, :], den_sb[0:128:32, :]).then_inc(den_spread, 16)
                sp.wait_ge(inverted, s + 1)
                sp.dma_start(inv_dram[:, :], inv_flat[:, :]).then_inc(inv_stored, 16)
                sp.wait_ge(inv_stored, s * 16 + 16)
                for h in range(2):
                    sp.dma_start(inv_sb[h * D:(h + 1) * D, :],
                                 inv_dram[h * 64:(h + 1) * 64, :].rearrange("(a p) n -> a (p n)", a=1)
                                 .partition_broadcast(D).rearrange("p a n -> p (a n)")).then_inc(inv_loaded, 16)

            def double(p, v):
                sp.wait_ge(rounded, v * 4 + 2)
                for h in range(2):
                    sp.dma_start(k_round[p][h][D:128, :].bitcast(F32), k_round[p][h][0:D, :].bitcast(F32)).then_inc(k_doubled, 16)
                sp.wait_ge(rounded, v * 4 + 4)
                for h in range(2):
                    sp.dma_start(q_max[p][h][0:D, :].bitcast(F32), q_full[p][h][0:D, :].bitcast(F32)).then_inc(q_doubled[p], 16)

            def max_rows(p, v):
                sp.wait_ge(rows_made, v + 1)
                for h in range(2):
                    sp.dma_start(q_max[p][h][D:D + 1, :].bitcast(F32).rearrange("a (c n) -> a c n", c=KCH),
                                 neg_max[:, h, :].bitcast(F32)).then_inc(rows_loaded, 16)

            def sp_step(s, p):
                max_rows(1 - p, s + 1)
                double(p, s + 2)
                spread(s)

            sp.wait_ge(pads_made, 1)
            double(0, 0)
            max_rows(0, 0)
            double(1, 1)
            sp_step(0, 0)
            with sp.Fori(1, STEPS - 4, 2) as it:
                sp_step(it, 1)
                sp_step(it + 1, 0)
            sp_step(STEPS - 3, 1)
            sp.wait_ge(v_staged, STEPS)
            for e in range(0, E, 2):
                sp.dma_start(raw_fc1[:, e:e + 2], fc1_w[e:e + 2].rearrange("e (r p) c -> p e r c", p=128)).then_inc(fc_loaded, 16)
                sp.dma_start(raw_fc2[:, e:e + 2], fc2_w[e:e + 2].rearrange("e d (r c) -> d e r c", c=C)).then_inc(fc_loaded, 16)
            sp_step(STEPS - 2, 0)
            for d in range(DUOS):
                sp.wait_ge(out_made, d + 1)
                sp.dma_start(out_d[d // (DUOS // B), d % (DUOS // B)], out_sb[d % 2]).then_inc(out_stored[d % 2], 16)
            for stored in out_stored:
                sp.wait_ge(stored, 16 * DUOS // 2)

        @block.tensor
        def _(pe):
            def keep_warm(count, to):
                for _ in range(count):
                    pe.matmul(to[:, 0:128], ident[:, :], ident[:, :], start=True, stop=True)

            pe.wait_ge(consts_made, 1)
            keep_warm(WARM_START, bank(6))
            pe.wait_ge(tables_loaded, 32)
            pe.transpose(bank(2)[:, 0:VOCAB], emb_sb[:, :], ident[0:VOCAB, 0:VOCAB])
            pe.wait_ge(diag_made, TAPS)
            for t in range(TAPS):
                last = pe.transpose(bank(2)[:, (t + 1) * C:(t + 2) * C], conv_diag[:, t, :], ident[:, :])
            last.then_inc(turned, 1)
            pe.wait_ge(tables_sb, 3)
            pe.matmul(bank(3)[:, 0:TAPS * C], embT[:, :], convT[:, :], start=True, stop=True).then_inc(folded_ready, 1)

            def conv(b):
                pe.wait_ge(onehot_made, b + 2)
                for g in range(b * NG // B, (b + 1) * NG // B):
                    for j in range(GROUP):
                        c0 = (g * GROUP + j) * CHUNK - b * S
                        for t in range(TAPS):
                            last = pe.matmul(bank(CONV_BANK[g])[:, j * C:(j + 1) * C], onehot[:, b, c0 + t:c0 + t + CHUNK],
                                             folded[:, t * C:(t + 1) * C], start=(t == 0), stop=(t == TAPS - 1))
                    last.then_inc(conv_filled, 1)

            pe.wait_ge(folded_sb, 1)
            conv(0)
            pe.wait_ge(w_loaded, 64)
            for w, k in enumerate((4, 5, 2)):
                for r in range(PAIRS):
                    last = pe.transpose(bank(k)[:, r * 128:(r + 1) * 128], raw_w[:, w, r, :], ident[:, :])
                last.then_inc(turned, 1)
            conv(1)

            for r in range(PAIRS):
                last = pe.transpose(bank(3)[:, r * C:(r + 1) * C], raw_wo[:, r, :], ident[:, :])
            last.then_inc(turned, 1)
            pe.wait_ge(small_loaded, 16 * 8)
            pe.wait_ge(weights_sb, 1)
            for i in range(2):
                pe.transpose(bank(4)[:, i * C:(i + 1) * C], raw_small[:, i, :], ident[:, :])
            pe.transpose(bank(4)[:, 2 * C:2 * C + 43], raw_bias[:, :], ident[0:43, 0:43]).then_inc(turned, 1)

            def x_to_features(g):
                for j in range(GROUP):
                    last = pe.transpose(bank(CONV_BANK[g])[:, j * CHUNK:(j + 1) * CHUNK], x1[:, g * GROUP + j, :], ident[:, :])
                last.then_inc(xt_filled, 1)

            def values(t):
                if t < 2:
                    pe.wait_ge(x_rest, NG)
                    pe.wait_ge(wv_rest, 1)
                else:
                    pe.wait_ge(v_sb, t - 1)
                rows = slice(t * CHUNK, (t + 1) * CHUNK)
                for i, (xs, ws) in enumerate(((xR, wvR), (xL, wvR), (xR, wvL))):
                    last = pe.matmul(bank(6 + t % 2), xs[:, rows], ws[:, :], start=(i == 0), stop=(i == 2))
                last.then_inc(v_filled, 1)

            pe.wait_ge(x_normed, KCH)
            for g in range(NG // B):
                x_to_features(g)

            def prep_item(item, slot, p, v, token0):
                kind = item[0]
                if kind in "qk":
                    if kind == "k":
                        pe.wait_ge(w_staged, v * 2 + 2)
                    w = "qk".index(kind)
                    for half in range(2):
                        cols = bass.ds(token0 + half * BANK, BANK)
                        for i, (ws, xs) in enumerate(((w_stR, xR), (w_stL, xR), (w_stR, xL))):
                            last = pe.matmul(slot[:, half * BANK:(half + 1) * BANK], ws[:, w, :], xs[:, cols],
                                             start=(i == 0), stop=(i == 2))
                elif kind == "max":
                    _, h, qc = item
                    if h == 0 and qc == 0:
                        pe.wait_ge(k_doubled, v * 32 + 32)
                        pe.wait_ge(split, v * 4 + 4)
                    for half in range(2):
                        cols = slice(half * BANK, (half + 1) * BANK)
                        last = pe.matmul(slot[:, cols], q_full[p][h][:, qc * CHUNK:(qc + 1) * CHUNK],
                                         k_round[p][h][:, cols], start=True, stop=True)
                else:
                    pe.wait_ge(maxed, v * 2 * KCH + 2 * KCH)
                    for h in range(2):
                        last = pe.transpose(slot[0:KCH, h * BANK:h * BANK + CHUNK], maxes[h][:, :], ident[:, :])
                last.then_inc(filled, 1)

            def wo_half(b, half, slot):
                for j in range(half * GROUP, (half + 1) * GROUP):
                    for r in range(PAIRS):
                        last = pe.matmul(slot[:, j * C:(j + 1) * C], attn_out[:, b * PAIRS + r, j * CHUNK:(j + 1) * CHUNK],
                                         woT[:, r, :], start=(r == 0), stop=(r == PAIRS - 1))
                return last

            def norm_transposed(b, slot):
                pe.wait_ge(n2_made, KCH * (b + 1))
                for j in range(KCH):
                    last = pe.transpose(slot[:, j * CHUNK:(j + 1) * CHUNK], normed2[:, j, :], ident[:, :])
                return last

            def xa_half(b, half, slot):
                cols = slice(half * BANK, (half + 1) * BANK)
                if half == 0:
                    pe.wait_ge(normT_made, b + 1)
                    pe.wait_ge(n1_made, KCH * (b + 1))
                pe.matmul(slot[:, cols], attn_wT, normT[:, cols], start=True, stop=False, skip_group_check=True)
                for j in range(half * GROUP, (half + 1) * GROUP):
                    last = pe.matmul(slot[:, j * CHUNK:(j + 1) * CHUNK], h1n[:, j, :], ident[:, :],
                                     start=False, stop=True, skip_group_check=True)
                return last

            def ffn_item(item, slot):
                kind = item[0]
                if kind == "wo":
                    pe.wait_ge(normalised, PAIRS)
                    wo_half(0, 0, slot)
                    last = wo_half(0, 1, slot)
                elif kind == "nt":
                    last = norm_transposed(0, slot)
                elif kind == "xa":
                    xa_half(0, 0, slot)
                    last = xa_half(0, 1, slot)
                else:
                    if item[1] == 0:
                        pe.wait_ge(fc_loaded, 16 * E)
                    for w, raw in enumerate((raw_fc1, raw_fc2)):
                        for r in range(HC):
                            last = pe.transpose(slot[:, w * BANK + r * C:w * BANK + (r + 1) * C], raw[:, item[1], r, :],
                                                ident[:, :])
                last.then_inc(filled, 1)

            def pe_step(s, p, prepare, s_is_first=False):
                token0 = (((s + 2) // PAIRS) % B) * S if prepare else 0
                if s_is_first:
                    earlier = PROLOGUE
                else:
                    earlier = [(i, s - 1) for i, n in numbered(True) if n is not None]
                emptied = [release(i, es) for i, es in earlier[-SLOTS:]]
                for item, n in numbered(prepare):
                    if n is None:
                        _, kc, half = item
                        if half == 0:
                            pe.wait_ge(exped, s * 2 * KCH + (2 * kc + 2))
                            if kc == 0:
                                pe.wait_ge(v_staged, s + 1)
                                if not s_is_first:
                                    pe.wait_ge(o_copied, s)
                        cols = slice(half * BANK, (half + 1) * BANK)
                        for h in range(2):
                            last = pe.matmul(acc_o[h * D:(h + 1) * D, cols], v_st[p][:, kc, h * D:(h + 1) * D],
                                             probs[h][kc % 2][:, cols], start=(kc == 0), stop=(kc == KCH - 1))
                        last.then_inc(pv_done, 1)
                        continue
                    slot = slots[slot_of(n)]
                    pe.wait_ge(*emptied[n])
                    emptied.append(release(item, s))
                    if item[0] == "exp":
                        _, kc, h = item
                        if kc == 0:
                            pe.wait_ge(q_doubled[p], (s - p) * 16 + 32)
                            pe.wait_ge(rows_loaded, s * 32 + 32)
                        keys = slice(kc * CHUNK, (kc + 1) * CHUNK)
                        for i, (ks, qs) in enumerate(((k_round, q_full), (k_rest, q_max))):
                            for half in range(2):
                                cols = slice(half * BANK, (half + 1) * BANK)
                                last = pe.matmul(slot[:, cols], ks[p][h][:, keys], qs[p][h][:, cols],
                                                 start=(i == 0), stop=(i == 1))
                        last.then_inc(filled, 1)
                    elif item[0] in ("den", "last den"):
                        for h in range(2):
                            pe.wait_ge(summed[h], (s + 1) * (KCH - 1))
                        for half in range(2):
                            for h in range(2):
                                quad = 32 * (2 * h + half)
                                to = slot[quad:quad + 32, 0:BANK] if item[0] == "den" else \
                                    slot[h * D:(h + 1) * D, half * BANK:(half + 1) * BANK]
                                last = pe.matmul(to, ones[:, 0:32 if item[0] == "den" else D],
                                                 sums[h][:, half * BANK:(half + 1) * BANK], start=True, stop=True)
                        last.then_inc(filled, 1)
                    elif item[0] in ("wo", "nt", "xa", "fct"):
                        ffn_item(item, slot)
                    else:
                        prep_item(item, slot, parity(item, p), target(item, s), token0)

            emptied = []
            for n, (item, s) in enumerate(PROLOGUE):
                if n == 0:
                    pe.wait_ge(x_rest, NG // B)
                elif n == 1:
                    pe.wait_ge(weights_sb, 5)
                    pe.wait_ge(wv_rest, 1)
                elif n == 2:
                    keep_warm(WARM_SPLIT, bank(5))
                    pe.wait_ge(small_sb, 1)
                    pe.wait_ge(pads_made, 1)
                if n >= SLOTS:
                    pe.wait_ge(*emptied[n - SLOTS])
                emptied.append(release(item, s))
                prep_item(item, slots[n % SLOTS], target(item, s) % 2, target(item, s), 0)
                if n == V_FROM - 1:
                    pe.wait_ge(x_late_normed, 1)
                    for g in range(NG // B, NG):
                        x_to_features(g)
                for t in values_after(n):
                    values(t)
            pe_step(0, 0, True, s_is_first=True)
            with pe.Fori(1, STEPS - 2, 2) as it:
                pe_step(it, 1, True)
                pe_step(it + 1, 0, True)
            pe_step(STEPS - 1, 1, False)

            def hidden(d):
                if d == 0:
                    pe.wait_ge(fct_sb[0], EARLY)
                    pe.wait_ge(fct_sb[1], 1)
                    pe.wait_ge(xa_made, 2)
                elif d == 1:
                    pe.wait_ge(inverted, STEPS + 1)
                elif d in (DUOS // B, DUOS // B + DUOS // B // 2):
                    pe.wait_ge(xa_made, 2 + 1 + (d > DUOS // B))
                if d >= 2:
                    pe.wait_ge(hid_made, 2 * HC * (d - 1))
                slot = duo_slots[d % 2][:, :].rearrange("p (e r n) -> p e r n", e=2, r=HC)
                for i in range(2):
                    b, e = d // (DUOS // B), d % (DUOS // B) * 2 + i
                    toks = slice(b * S + e * CHUNK, b * S + (e + 1) * CHUNK)
                    for r in range(HC):
                        last = pe.matmul(slot[:, i, r], fcT[:, e, 0, r, :], xaT[:, toks], start=True, stop=True)
                last.then_inc(hid_filled, 1)

            def second(d):
                pe.wait_ge(hid_made, 2 * HC * (d + 1))
                if d >= 2:
                    pe.wait_ge(z_biased, d - 1)
                for i in range(2):
                    e = d % (DUOS // B) * 2 + i
                    o = (d % 2) * BANK + i * CHUNK
                    for r in range(HC):
                        last = pe.matmul(acc_o[:, o:o + CHUNK], fcT[:, e, 1, r, :], hidT[d % 2][:, i, r, :],
                                         start=(r == 0), stop=(r == HC - 1))
                last.then_inc(y_filled, 1)

            def third(d):
                pe.wait_ge(y_made, d + 1)
                for i in range(2):
                    o = (d % 2) * BANK + 2 * CHUNK + i * C
                    last = pe.matmul(acc_o[:, o:o + C], yT[d % 2][:, i * CHUNK:(i + 1) * CHUNK], next_wT,
                                     start=True, stop=True)
                last.then_inc(z_filled, 1)

            hidden(0)
            pe.wait_ge(fct_sb[1], E - EARLY)
            for half in range(2):
                pe.wait_ge(normalised, STEPS + half)
                wo_half(1, half, late_slot).then_inc(wo_filled, 1)
            second(0)
            hidden(1)
            norm_transposed(1, late_slot).then_inc(nt_filled, 1)
            third(0)
            for half in range(2):
                xa_half(1, half, late_slot).then_inc(xa_filled, 1)
            for d in range(2, DUOS + 2):
                if d < DUOS:
                    hidden(d)
                if d >= 3:
                    third(d - 2)
                if d - 1 < DUOS:
                    second(d - 1)

        @block.scalar
        def _(act):
            act.dma_start(emb_sb[:, :], emb).then_inc(tables_loaded, 16)
            act.dma_start(conv_sb[:, :, :], conv_w).then_inc(tables_loaded, 16)
            act.dma_start(raw_w[:, 0], wq.rearrange("(r p) c -> p r c", p=128)).then_inc(w_loaded, 16)
            act.dma_start(raw_w[:, 1], wk.rearrange("(r p) c -> p r c", p=128)).then_inc(w_loaded, 16)
            act.wait_ge(consts_made, 1)
            act.activation(table_warmer[:, 0:1], eps[:, 0:1], ACT.Sqrt)

            def relu(g):
                act.wait_ge(conv_filled, g + 1)
                act.activation(h0[:, g * GROUP:(g + 1) * GROUP, :],
                               bank(CONV_BANK[g]).rearrange("p (t c) -> p t c", c=C), ACT.Relu).then_inc(h0_made, 1)

            def x_round(g):
                act.wait_ge(xt_filled, g + 1)
                act.copy(xR[:, g * BANK:(g + 1) * BANK], bank(CONV_BANK[g])).then_inc(x_rounded, 1)

            def x_sqrt(b):
                act.wait_ge(x_aggr, KCH * (b + 1))
                act.activation(std[:, 0, :], mv[:, :, 1], ACT.Sqrt, bias=eps[:, 0:1]).then_inc(x_std, 1)

            relu(0)
            relu(1)
            for w, k in enumerate((4, 5)):
                act.wait_ge(turned, 2 + w)
                act.copy(wqk[:, :, w, :], bank(k).rearrange("c (r n) -> c r n", n=128)).then_inc(weights_sb, 1)
            act.wait_ge(turned, 4)
            act.copy(wvR[:, :], bank(2)).then_inc(weights_sb, 1)
            x_sqrt(0)
            relu(2)
            relu(3)
            act.wait_ge(turned, 5)
            act.copy(woT[:, :, :], bank(3).rearrange("p (r c) -> p r c", c=C)).then_inc(weights_sb, 2)
            x_round(0)
            x_round(1)

            def act_item(item, count, slot, p, s, first):
                kind = item[0]
                if kind == "exp":
                    _, kc, h = item
                    act.wait_ge(filled, count)
                    if not (first and kc < 2):
                        act.wait_ge(pv_done, s * 2 * KCH + 2 * (kc - 1))
                        act.wait_ge(summed[h], s * (KCH - 1) + adds_before_reuse(kc))
                    act.activation(probs[h][kc % 2][:, :], slot[:, :], ACT.Exp, scale=SCALE).then_inc(exped, 1)
                elif kind in "qk":
                    act.wait_ge(filled, count)
                    for h in range(2):
                        act.copy((q_full if kind == "q" else k_round)[p][h][0:D, :],
                                 slot[h * D:(h + 1) * D, :]).then_inc(rounded, 1)
                elif kind == "den":
                    act.wait_ge(pv_done, s * 2 * KCH + 2 * KCH)
                    if not first:
                        act.wait_ge(normalised, s)
                    act.copy(o_sb[:, :], acc_o[:, :]).then_inc(o_copied, 1)
                    act.wait_ge(filled, count)
                    act.copy(den_sb[:, :], slot[:, 0:BANK]).then_inc(den_copied, 1)
                elif kind == "nt":
                    act.wait_ge(filled, count)
                    norm_t(0, slot)
                elif kind == "xa":
                    act.wait_ge(filled, count)
                    for half in range(2):
                        xa_copy(0, half, slot)
                elif kind == "fct":
                    if item[1] == 0:
                        ln_sqrt(0)
                    if item[1] >= EARLY:
                        act.wait_ge(filled, count)
                        act.copy(fcT[:, item[1], :, :, :],
                                 slot[:, :].rearrange("p (w r c) -> p w r c", w=2, c=C)).then_inc(fct_sb[1], 1)

            def ln_sqrt(b):
                act.wait_ge(ln_aggr, KCH * (b + 1))
                act.activation(std[:, 0, :], mv[:, :, 1], ACT.Sqrt, bias=eps[:, 0:1]).then_inc(ln_std, 1)
                act.activation(std[:, 1, :], mv[:, :, 1], ACT.Sqrt, scale=1.0 + EPS,
                               bias=eps_squared[:, 0:1]).then_inc(ln_std, 1)

            def norm_t(b, slot):
                act.activation(normT[:, :], slot[:, :], ACT.Identity, bias=b_col, scale=g_col).then_inc(normT_made, 1)

            def xa_copy(b, half, slot):
                act.activation(xaT[:, b * S + half * BANK:b * S + (half + 1) * BANK], slot[:, half * BANK:(half + 1) * BANK],
                               ACT.Identity, bias=attn_b_col).then_inc(xa_made, 1)

            def act_step(s, p, prepare, first=False):
                for item, n in numbered(prepare):
                    if n is not None:
                        act_item(item, item_count(s, n), slots[slot_of(n)], parity(item, p), s, first)

            act.wait_ge(pads_made, 1)
            for n, (item, s) in enumerate(PROLOGUE):
                act_item(item, n + 1, slots[n % SLOTS], target(item, s) % 2, s, True)
                if n == 0:
                    x_sqrt(1)
                elif n == 1:
                    act.activation(table_warmer[:, 1:2], eps[:, 0:1], ACT.Exp)
                if n == V_FROM - 1:
                    x_round(2)
                    x_round(3)
                for t in values_after(n):
                    b, kc = divmod(t, KCH)
                    act.wait_ge(v_filled, t + 1)
                    act.copy(v_all[:, b * PAIRS:(b + 1) * PAIRS, kc, :],
                             bank(6 + t % 2).rearrange("p (r d) -> p r d", r=PAIRS)).then_inc(v_sb, 1)
            act_step(0, 0, True, first=True)
            with act.Fori(1, STEPS - 2, 2) as it:
                act_step(it, 1, True)
                act_step(it + 1, 0, True)
            act_step(STEPS - 1, 1, False)

            def gelu_hidden(d):
                act.wait_ge(hid_filled, d + 1)
                if d >= 2:
                    act.wait_ge(y_filled, d - 1)
                slot = duo_slots[d % 2][:, :].rearrange("p (e r n) -> p e r n", e=2, r=HC)
                for i in range(2):
                    e = d % (DUOS // B) * 2 + i
                    for r in range(HC):
                        act.activation(hidT[d % 2][:, i, r, :], slot[:, i, r], ACT.Gelu,
                                       bias=fc1_b_col[:, e * HC + r:e * HC + r + 1]).then_inc(hid_made, 1)

            def gelu_z(d):
                act.wait_ge(z_biased, d + 1)
                if d >= 2:
                    act.wait_ge(out_made, d - 1)
                act.activation(z_act[d % 2], z_pre[d % 2], ACT.Gelu).then_inc(z_made, 1)

            gelu_hidden(0)
            ln_sqrt(1)
            act.wait_ge(nt_filled, 1)
            norm_t(1, late_slot)
            gelu_hidden(1)
            for half in range(2):
                act.wait_ge(xa_filled, half + 1)
                xa_copy(1, half, late_slot)
            for d in range(2, DUOS + 2):
                if d < DUOS:
                    gelu_hidden(d)
                gelu_z(d - 2)

        @block.vector
        def _(dve):
            dve.wait_ge(consts_made, 1)
            dve.tensor_copy(iota_f[:, :], iota_i[:, :]).then_inc(iota_cast, 1)
            dve.memset(onehot[:, :, 0:1], 0.0).then_inc(onehot_made, 1)
            dve.wait_ge(tables_loaded, 32)
            for t in range(TAPS):
                dve.tensor_tensor(conv_diag[:, t, :].rearrange("o (g i) -> o g i", i=4),
                                  conv_sb[:, :, t].unsqueeze(1).broadcast_to([C, 32, 4]),
                                  group_mask[:, :].unsqueeze(2).broadcast_to([C, 32, 4]), ALU.mult).then_inc(diag_made, 1)
            dve.wait_ge(iota_cast, 1)
            dve.wait_ge(ids_loaded, 16 * B)
            for b in range(B):
                dve.tensor_scalar(onehot[:, b, 1:S + 1], ids[:, b * S:(b + 1) * S], float(VOCAB - 1),
                                  iota_f[:, 0:1], ALU.min, ALU.is_equal).then_inc(onehot_made, 1)
            dve.wait_ge(turned, 1)
            dve.memset(embT[:, VOCAB:128], 0.0).then_inc(tables_sb, 1)
            dve.tensor_copy(embT[:, 0:VOCAB], bank(2)[:, 0:VOCAB]).then_inc(tables_sb, 1)
            dve.tensor_copy(convT[:, :], bank(2)[:, C:(TAPS + 1) * C]).then_inc(tables_sb, 1)
            dve.wait_ge(folded_ready, 1)
            dve.tensor_copy(folded[:, :], bank(3)[:, 0:TAPS * C]).then_inc(folded_sb, 1)

            def x_statistics(b):
                for j in range(KCH):
                    if j % GROUP == 0:
                        dve.wait_ge(h0_made, (b * KCH + j) // GROUP + 1)
                    dve.bn_stats(stats[:, j, :], h0[:, b * KCH + j, :]).then_inc(x_stats, 1)
                if b:
                    dve.wait_ge(x_normed, KCH)
                for j in range(KCH):
                    dve.wait_ge(x_stats, KCH * b + j + 1)
                    dve.bn_aggr(mv[:, j, :], stats[:, j, :]).then_inc(x_aggr, 1)

            def x_inverse(b):
                dve.wait_ge(x_std, b + 1)
                dve.reciprocal(rstd[:, 0, :], std[:, 0, :]).then_inc(x_rstd, 1)

            def x_rests(g):
                dve.wait_ge(x_rounded, g + 1)
                dve.tensor_tensor(xL[:, g * BANK:(g + 1) * BANK], bank(CONV_BANK[g]),
                                  xR[:, g * BANK:(g + 1) * BANK].bitcast(F32), ALU.subtract).then_inc(x_rest, 1)

            def stage_w(v):
                src = wqk[:, v % PAIRS, :, :]
                dve.tensor_copy(w_stR[:, :, :], src).then_inc(w_staged, 1)
                dve.wait_ge(w_staged, v * 2 + 1)
                dve.tensor_tensor(w_stL[:, :, :], src, w_stR[:, :, :].bitcast(F32), ALU.subtract).then_inc(w_staged, 1)

            def dve_item(item, count, slot, p, s, first=False):
                kind = item[0]
                if kind == "exp":
                    _, kc, h = item
                    if h == 1 and kc >= POOL_ADDS:
                        dve.wait_ge(exped, s * 2 * KCH + (2 * kc + 1))
                        dve.wait_ge(summed[0], s * (KCH - 1) + (kc - 1))
                        dve.tensor_tensor(sums[0][:, :], sums[0][:, :], probs[0][kc % 2][:, :], ALU.add).then_inc(summed[0], 1)
                elif kind in "qk":
                    whole = q_full if kind == "q" else k_round
                    for h in range(2):
                        rest = q_full[p][h][D:128, :] if kind == "q" else k_rest[p][h][0:D, :]
                        dve.wait_ge(rounded, target(item, s) * 4 + (h + (1 if kind == "k" else 3)))
                        dve.tensor_tensor(rest, slot[h * D:(h + 1) * D, :], whole[p][h][0:D, :].bitcast(F32),
                                          ALU.subtract).then_inc(split, 1)
                elif kind == "max":
                    _, h, qc = item
                    dve.wait_ge(filled, count)
                    dve.reduce_max(maxes[h][:, qc:qc + 1], slot[:, :], AX.X).then_inc(maxed, 1)
                elif kind == "rows":
                    dve.wait_ge(filled, count)
                    if not first:
                        dve.wait_ge(rows_loaded, target(item, s) * 32)
                    dve.tensor_scalar(neg_max[:, :, :], slot[0:KCH, :].rearrange("c (h n) -> c h n", h=2)[:, :, 0:CHUNK],
                                      -1.0, None, ALU.mult).then_inc(rows_made, 1)
                elif kind == "wo":
                    dve.wait_ge(filled, count)
                    for half in range(2):
                        add_and_stats(0, half, slot)
                elif kind == "fct" and item[1] < EARLY:
                    if item[1] == 0:
                        dve.wait_ge(w_staged, 2 * (STEPS + 1))
                        dve.wait_ge(split, 4 * (STEPS + 1))
                        dve.wait_ge(k_doubled, 32 * (STEPS + 1))
                        dve.wait_ge(q_doubled[0], 32 * (STEPS // 2 + 1))
                    dve.wait_ge(filled, count)
                    dve.tensor_copy(fcT[:, item[1], :, :, :],
                                    slot[:, :].rearrange("p (w r c) -> p w r c", w=2, c=C)).then_inc(fct_sb[0], 1)
                    if item[1] < 2:
                        norms(0, item[1] == 0, item[1] == 1)
                elif kind == "last den":
                    dve.wait_ge(filled, count)
                    dve.wait_ge(normalised, STEPS - 1)
                    for half in range(2):
                        cols = slice(half * BANK, (half + 1) * BANK)
                        dve.reciprocal(inv_sb[:, cols], slot[:, cols]).then_inc(inverted, 1)
                        dve.wait_ge(inverted, STEPS + half)
                        if half == 0:
                            dve.wait_ge(pv_done, STEPS * 2 * KCH)
                        dve.tensor_tensor(attn_out[:, STEPS - 1, cols], acc_o[:, cols], inv_sb[:, cols],
                                          ALU.mult).then_inc(normalised, 1)

            def invert(s):
                dve.wait_ge(den_spread, s * 16 + 16)
                dve.reciprocal(inv_flat[:, :], den_flat[:, :]).then_inc(inverted, 1)

            def add_and_stats(b, half, slot):
                own = range(half * GROUP, (half + 1) * GROUP)
                chunks = slice(b * KCH + half * GROUP, b * KCH + (half + 1) * GROUP)
                if b == 0 and half == 0:
                    dve.wait_ge(residual_made, NG)
                if b == 1 and half == 0:
                    dve.wait_ge(n1_made, KCH)
                dve.tensor_tensor(residual[:, chunks, :], slot[:, half * BANK:(half + 1) * BANK]
                                  .rearrange("p (t c) -> p t c", c=C), residual[:, chunks, :], ALU.add).then_inc(h1_made, 1)
                dve.wait_ge(h1_made, 2 * b + half + 1)
                for j in own:
                    dve.bn_stats(stats[:, j, :], residual[:, b * KCH + j, :]).then_inc(ln_stats, 1)
                for j in own:
                    dve.wait_ge(ln_stats, b * KCH + j + 1)
                    dve.bn_aggr(mv[:, j, :], stats[:, j, :]).then_inc(ln_aggr, 1)

            def norms(b, first, second):
                if first:
                    dve.wait_ge(ln_std, 2 * (b + 1))
                    dve.reciprocal(rstd[:, :, :], std[:, :, :]).then_inc(ln_rstd, 1)
                    dve.wait_ge(ln_rstd, b + 1)
                    if b == 1:
                        dve.wait_ge(xa_made, 2)
                for which, dst, done in [(1, normed2, n2_made)] * first + [(0, h1n, n1_made)] * second:
                    for j in range(KCH):
                        dve.tensor_scalar(dst[:, j, :], residual[:, b * KCH + j, :], mv[:, j, 0:1], rstd[:, which, j:j + 1],
                                          ALU.subtract, ALU.mult).then_inc(done, 1)

            def stage_v(v, p):
                dve.tensor_copy(v_st[p][:, :, :], v_all[:, v, :, :]).then_inc(v_staged, 1)

            def dve_step(s, p, prepare, first=False):
                items = list(numbered(prepare))
                if prepare:
                    k, rows = (next(i for i, (item, _) in enumerate(items) if item == (kind,)) for kind in ("k", "rows"))
                    items[k], items[rows] = items[rows], items[k]
                for item, n in items:
                    if item == ("pv", 0, 1):
                        if not first:
                            invert(s - 1)
                        if prepare:
                            if not first:
                                dve.wait_ge(pv_done, s * 2 * KCH)
                            stage_v(s + 1, 1 - p)
                    if n is not None:
                        dve_item(item, item_count(s, n), slots[slot_of(n)], parity(item, p), s)
                    if item == ("max", 0, 2):
                        stage_w(s + 2)

            x_statistics(0)
            dve.wait_ge(weights_sb, 3)
            dve.tensor_tensor(wvL[:, :], bank(2), wvR[:, :].bitcast(F32), ALU.subtract).then_inc(wv_rest, 1)
            x_inverse(0)
            dve.wait_ge(x_rstd, 1)
            for t in range(KCH):
                dve.tensor_scalar(x1[:, t, :], h0[:, t, :], mv[:, t, 0:1], rstd[:, 0, t:t + 1],
                                  ALU.subtract, ALU.mult).then_inc(x_normed, 1)
            stage_w(0)
            x_rests(0)
            x_rests(1)
            x_statistics(1)
            dve.wait_ge(pads_made, 1)
            for n, (item, s) in enumerate(PROLOGUE):
                dve_item(item, n + 1, slots[n % SLOTS], target(item, s) % 2, s, True)
                if n == 0:
                    x_inverse(1)
                elif n == 1:
                    dve.wait_ge(turned, 6)
                    dve.tensor_copy(small[:, :], bank(4)[:, 0:2 * C + 43]).then_inc(small_sb, 1)
                if n == V_FROM - 1:
                    x_rests(2)
                    x_rests(3)
                if item == ("max", 0, 2):
                    stage_w(1)
            dve.wait_ge(v_sb, NCH)
            stage_v(0, 0)
            dve_step(0, 0, True, first=True)
            with dve.Fori(1, STEPS - 2, 2) as it:
                dve_step(it, 1, True)
                dve_step(it + 1, 0, True)
            dve_step(STEPS - 1, 1, False)

            def y_bias(d):
                e = d % (DUOS // B) * 2
                dve.wait_ge(y_filled, d + 1)
                dve.tensor_tensor(yT[d % 2].rearrange("c (e n) -> c e n", e=2),
                                  acc_o[:, (d % 2) * BANK:(d % 2) * BANK + 2 * CHUNK].rearrange("c (e n) -> c e n", e=2),
                                  fc2_b_col[:, e:e + 2].unsqueeze(2).broadcast_to([C, 2, CHUNK]), ALU.add).then_inc(y_made, 1)

            def z_bias(d):
                dve.wait_ge(z_filled, d + 1)
                if d >= 2:
                    dve.wait_ge(z_made, d - 1)
                dve.tensor_tensor(z_pre[d % 2],
                                  acc_o[:, (d % 2) * BANK + 2 * CHUNK:(d % 2 + 1) * BANK].rearrange("p (e c) -> p e c", e=2),
                                  next_b_row[:, :].unsqueeze(1).broadcast_to([128, 2, C]), ALU.add).then_inc(z_biased, 1)

            for half in range(2):
                dve.wait_ge(wo_filled, half + 1)
                add_and_stats(1, half, late_slot)
            y_bias(0)
            norms(1, True, True)
            z_bias(0)
            y_bias(1)
            for d in range(2, DUOS + 1):
                z_bias(d - 1)
                if d < DUOS:
                    y_bias(d)

        @block.gpsimd
        def _(pool):
            pool.memset(ident[:, :], 0.0).then_inc(zeroed, 1)
            pool.memset(group_mask[:, :], 1.0).then_inc(zeroed, 1)
            pool.memset(ones[:, :], 1.0)
            pool.memset(eps[:, :], EPS)
            pool.memset(eps_squared[:, :], EPS * EPS)
            pool.iota(iota_i[:, :], pattern=[[0, 1]], base=0, channel_multiplier=1)
            pool.wait_ge(zeroed, 2)
            pool.affine_select(out=group_mask[:, :], in_=group_mask[:, :], compare_op=ALU.is_ge, fill=0.0, base=0,
                               pattern=[[-4, 32]], channel_multiplier=1).then_inc(zeroed, 1)
            pool.wait_ge(zeroed, 3)
            pool.affine_select(out=group_mask[:, :], in_=group_mask[:, :], compare_op=ALU.is_ge, fill=0.0, base=3,
                               pattern=[[4, 32]], channel_multiplier=-1)
            pool.affine_select(out=ident[:, :], in_=ident[:, :], compare_op=ALU.not_equal, fill=1.0, base=0,
                               pattern=[[-1, 128]], channel_multiplier=1).then_inc(consts_made, 1)
            for p in range(2):
                for h in range(2):
                    pool.memset(q_max[p][h][:, :].bitcast(F32), 0.0)
                    last = pool.memset(k_rest[p][h][:, :].bitcast(F32), 1.0)
            last.then_inc(pads_made, 1)

            late = slice(KCH, 2 * KCH)
            pool.wait_ge(x_aggr, 2 * KCH)
            pool.tensor_tensor(x1[:, late, :], h0[:, late, :], mv[:, :, 0:1].broadcast_to([128, KCH, C]),
                               ALU.subtract).then_inc(x_centred, 1)
            pool.wait_ge(x_rstd, 2)
            pool.wait_ge(x_centred, 1)
            pool.tensor_tensor(x1[:, late, :], x1[:, late, :], rstd[:, 0, :].unsqueeze(2).broadcast_to([128, KCH, C]),
                               ALU.mult).then_inc(x_late_normed, 1)
            pool.wait_ge(x_late_normed, 1)
            pool.wait_ge(x_normed, KCH)
            pool.wait_ge(onehot_made, B + 1)
            for g in range(NG):
                own = slice(g * GROUP, (g + 1) * GROUP)
                pool.tensor_tensor(residual[:, own, :], h0[:, own, :], x1[:, own, :], ALU.add).then_inc(residual_made, 1)

            def normalise(s):
                pool.wait_ge(inv_loaded, s * 32 + 32)
                pool.tensor_tensor(attn_out[:, s, :], o_sb[:, :], inv_sb[:, :], ALU.mult).then_inc(normalised, 1)

            def pool_step(s, p, prepare, first=False):
                for kc in range(1, KCH):
                    if kc == 6 and not first:
                        normalise(s - 1)
                    for h in range(2):
                        if h == 0 and kc >= POOL_ADDS:
                            continue
                        pool.wait_ge(exped, s * 2 * KCH + (2 * kc + h + 1))
                        if kc == 1 and not first:
                            pool.wait_ge(den_copied, s)
                        if kc > 1:
                            pool.wait_ge(summed[h], s * (KCH - 1) + (kc - 1))
                        before = probs[h][0] if kc == 1 else sums[h]
                        pool.tensor_tensor(sums[h][:, :], before[:, :], probs[h][kc % 2][:, :], ALU.add).then_inc(summed[h], 1)

            pool_step(0, 0, True, first=True)
            with pool.Fori(1, STEPS - 2, 2) as it:
                pool_step(it, 1, True)
                pool_step(it + 1, 0, True)
            pool_step(STEPS - 1, 1, False)

            for d in range(DUOS):
                chunk = d // (DUOS // B) * KCH + d % (DUOS // B) * 2
                pool.wait_ge(z_made, d + 1)
                if d >= 2:
                    pool.wait_ge(out_stored[d % 2], 16 * (d // 2))
                pool.tensor_tensor(out_sb[d % 2], z_act[d % 2], residual[:, chunk:chunk + 2, :], ALU.add).then_inc(out_made, 1)


_INS = ["x", "L0_tok_emb_table", "L0_tok_conv_w", "L0_attn_Wq", "L0_attn_Wk", "L0_attn_Wv", "L0_attn_Wo",
        "L0_ffn_ln_g", "L0_ffn_ln_b", "L0_ffn_attn_w", "L0_ffn_attn_b", "L0_ffn_fc1_w", "L0_ffn_fc1_b",
        "L0_ffn_fc2_w", "L0_ffn_fc2_b", "L0_ffn_next_w", "L0_ffn_next_b"]
_OUT = ((2, 1024, 128), "float32")


def kernel(**inputs):
    import numpy as np
    import concourse.bacc as bacc
    from concourse.bass_utils import run_bass_kernel_spmd

    nc = bacc.Bacc("TRN2", target_bir_lowering=False, num_devices=1)
    arrays, args = {}, []
    for name in _INS:
        a = np.ascontiguousarray(inputs[name])
        arrays[f"in_{name}"] = a
        args.append(nc.dram_tensor(f"in_{name}", a.shape, mybir.dt.from_np(a.dtype), kind="ExternalInput").ap())
    args.append(nc.dram_tensor("out_h", _OUT[0], mybir.dt.from_np(np.dtype(_OUT[1])), kind="ExternalOutput").ap())
    build(nc, *args)
    r = run_bass_kernel_spmd(nc, [arrays], core_ids=[0])
    return r.results[0]["out_h"]
```
